# Optimizing a Trainium2 kernel written in Bass

```python
import numpy as np
import jax
import jax.numpy as jnp

def _softmax(x, axis=-1):
    return jax.nn.softmax(x, axis=axis)

def _gelu(x):
    return jax.nn.gelu(x, approximate=True)

def _silu(x):
    return jax.nn.silu(x)

def _sigmoid(x):
    return jax.nn.sigmoid(x)

def _layernorm(x, axis=-1, eps=1e-05):
    m = jnp.mean(x, axis=axis, keepdims=True)
    v = jnp.var(x, axis=axis, keepdims=True)
    return (x - m) / jnp.sqrt(v + eps)

def _scatter_add(tgt, idx, src, axis=0):
    return tgt.at[idx].add(src)

def _segment_sum(src, seg, n):
    return jax.ops.segment_sum(src, seg, n)
kernel_name = 'mk_seq_postln_d1_jaxref_r8_56b916'

def setup_inputs(seed: int=0):
    np.random.seed(seed)
    _w = jnp.asarray

    def _L0_attn_setup():
        import jax, jax.numpy as jnp
        import numpy as np
        D_MODEL = 256
        N_QUERY = 4
        N_HEAD = 8
        D_HEAD = D_MODEL // (N_QUERY * N_HEAD)
        D_KV = D_HEAD * N_HEAD
        BATCH, SEQ = (2, 256)
        key = jax.random.key(seed)
        ks = jax.random.split(key, 5)
        w_scale = 1.0 / np.sqrt(D_MODEL).astype(np.float32)
        x = jax.random.normal(ks[0], (BATCH, SEQ, D_MODEL), jnp.float32)
        Wq = jax.random.normal(ks[1], (D_MODEL, D_MODEL), jnp.float32) * w_scale
        Wk = jax.random.normal(ks[2], (D_KV, D_MODEL), jnp.float32) * w_scale
        Wv = jax.random.normal(ks[3], (D_KV, D_MODEL), jnp.float32) * w_scale
        memory = jax.random.normal(ks[4], (D_KV, D_KV), jnp.float32) * 0.02
        memory_norm = jnp.ones((D_KV, 1), jnp.float32)
        memory_weight = jnp.ones((1,), jnp.float32)
        return dict(x=x, Wq=Wq, Wk=Wk, Wv=Wv, memory=memory, memory_norm=memory_norm, memory_weight=memory_weight)
    _L0_attn_in = _L0_attn_setup()

    def _L0_ffn_setup():
        import jax, jax.numpy as jnp
        import numpy as np
        D_MODEL = 256
        D_EXPERT = 1024
        EPS = 1e-08

        def ternary_quant(w):
            scale = jnp.mean(jnp.abs(w)) + EPS
            q = jnp.clip(jnp.round(w / scale), -1.0, 1.0) * scale
            return w + jax.lax.stop_gradient(q - w)
        key = jax.random.key(seed)
        k_x, k_up, k_gate, k_down = jax.random.split(key, 4)
        std_in = 1.0 / np.sqrt(D_MODEL)
        std_exp = 1.0 / np.sqrt(D_EXPERT)
        return {'x': jax.random.normal(k_x, (4, 256, D_MODEL), dtype=jnp.float32), 'W_up': jax.random.normal(k_up, (D_EXPERT, D_MODEL), dtype=jnp.float32) * std_in, 'W_gate': jax.random.normal(k_gate, (D_EXPERT, D_MODEL), dtype=jnp.float32) * std_in, 'W_down': jax.random.normal(k_down, (D_MODEL, D_EXPERT), dtype=jnp.float32) * std_exp}
    _L0_ffn_in = _L0_ffn_setup()
    _d = {'L0_attn_x': _L0_attn_in['x'], 'L0_attn_Wq': _L0_attn_in['Wq'], 'L0_attn_Wk': _L0_attn_in['Wk'], 'L0_attn_Wv': _L0_attn_in['Wv'], 'L0_attn_memory': _L0_attn_in['memory'], 'L0_attn_memory_norm': _L0_attn_in['memory_norm'], 'L0_attn_memory_weight': _L0_attn_in['memory_weight'], 'L0_ffn_W_up': _L0_ffn_in['W_up'], 'L0_ffn_W_gate': _L0_ffn_in['W_gate'], 'L0_ffn_W_down': _L0_ffn_in['W_down']}
    _x0 = _d['L0_attn_x']
    _d['L0_attn_x'] = jax.random.normal(jax.random.fold_in(jax.random.key(seed), 1), (2, 1024, 256), dtype=_x0.dtype)
    del _x0
    return _d

def reference(L0_attn_x, L0_attn_Wq, L0_attn_Wk, L0_attn_Wv, L0_attn_memory, L0_attn_memory_norm, L0_attn_memory_weight, L0_ffn_W_up, L0_ffn_W_gate, L0_ffn_W_down):

    def _L0_attn_ref(x, Wq, Wk, Wv, memory, memory_norm, memory_weight):
        import jax, jax.numpy as jnp
        import numpy as np
        D_MODEL = 256
        N_QUERY = 4
        N_HEAD = 8
        D_HEAD = D_MODEL // (N_QUERY * N_HEAD)
        D_KV = D_HEAD * N_HEAD
        BATCH, SEQ = (2, 256)
        b, s, d = x.shape
        q = x @ Wq.T
        k = x @ Wk.T
        v = x @ Wv.T
        qh = q.reshape(b, s, N_QUERY, N_HEAD, D_HEAD)
        kh = k.reshape(b, s, N_HEAD, D_HEAD)
        vh = v.reshape(b, s, N_HEAD, D_HEAD)
        scale = np.float32(1.0 / np.sqrt(np.float32(D_HEAD)))
        scores = jnp.einsum('bsqhd,bthd->bqhst', qh, kh) * scale
        probs = jax.nn.softmax(scores, axis=-1)
        a_dot = jnp.einsum('bqhst,bthd->bsqhd', probs, vh)
        a_dot = a_dot.reshape(b, s, N_QUERY * N_HEAD, D_HEAD)
        sigma_q = jax.nn.elu(q.reshape(b, s, N_QUERY, D_KV))
        a_mem = sigma_q @ memory / (sigma_q @ memory_norm)
        a_mem = a_mem.reshape(b, s, N_QUERY * N_HEAD, D_HEAD)
        w = jax.nn.sigmoid(memory_weight)
        out = a_dot * (1.0 - w) + a_mem * w
        return out.reshape(b, s, D_MODEL)

    def _L0_ffn_ref(x, W_up, W_gate, W_down):
        import jax, jax.numpy as jnp
        import numpy as np
        D_MODEL = 256
        D_EXPERT = 1024
        EPS = 1e-08

        def ternary_quant(w):
            scale = jnp.mean(jnp.abs(w)) + EPS
            q = jnp.clip(jnp.round(w / scale), -1.0, 1.0) * scale
            return w + jax.lax.stop_gradient(q - w)
        wu = ternary_quant(W_up)
        wg = ternary_quant(W_gate)
        wd = ternary_quant(W_down)
        up = jnp.einsum('bsd,ed->bse', x, wu)
        gate = jnp.einsum('bsd,ed->bse', x, wg)
        hidden = jax.nn.silu(up) * gate
        return jnp.einsum('bse,de->bsd', hidden, wd)
    x = L0_attn_x
    x = _layernorm(x + _L0_attn_ref(x, L0_attn_Wq, L0_attn_Wk, L0_attn_Wv, L0_attn_memory, L0_attn_memory_norm, L0_attn_memory_weight), axis=-1)
    x = _layernorm(x + _L0_ffn_ref(x, L0_ffn_W_up, L0_ffn_W_gate, L0_ffn_W_down), axis=-1)
    return x

_drawn_inputs = setup_inputs


def setup_inputs(seed=0):
    import zlib

    import numpy as np

    out = dict(_drawn_inputs(seed))
    spreads = {'L0_attn_memory_norm': (1.0, 0.2)}
    factors = {}
    for name, (base, spread) in spreads.items():
        noise = np.random.default_rng([zlib.crc32(name.encode()), seed]).standard_normal(out[name].shape)
        drawn = base * np.exp(spread * noise) if base else spread * noise
        out[name] = jnp.asarray(drawn.astype(out[name].dtype))
    for name, factor in factors.items():
        out[name] = (out[name] * factor).astype(out[name].dtype)
    return out
```

```python
from contextlib import ExitStack

import concourse.bass as bass
from concourse import mybir

F32 = mybir.dt.float32
BF16 = mybir.dt.bfloat16
FP16 = mybir.dt.float16
ALU = mybir.AluOpType
ACT = mybir.ActivationFunctionType
AX = mybir.AxisListType

P = 128
BATCH, SEQ, DM = 2, 1024, 256
NQ, NH, DH = 4, 8, 8
DKV = NH * DH
DE = 1024
SCALE = float(1.0 / (DH ** 0.5))
LN_EPS = 1e-5
Q_EPS = 1e-8
PIECES = 3
HALF = 512
CHUNKS = BATCH * SEQ // HALF
TPC = HALF // P
KC = DM // P
PROD_ROWS = PIECES * PIECES * DH
MAX_ROW = 96
ROWS = MAX_ROW + PIECES
TB = SEQ // P
HG = 4
ITERS = (SEQ // HALF) * NQ
QUADS = 4 * ITERS
TILES = TB * HG
PAIRS = HG * TPC
PSLOTS = 16
VW = 32
ER = DE // P
CONSTS = 9
FINE = 2.0 ** -11


def attention_ffn_kernel(nc, x, Wq, Wk, Wv, memory, memory_norm, memory_weight, W_up, W_gate, W_down, out):
    with ExitStack() as ctx:
        def sb(name, shape, dt=F32):
            return ctx.enter_context(nc.sbuf_tensor(name, shape, dt))

        def sem(name):
            return ctx.enter_context(nc.semaphore(name))

        xr = sb("xr", [P, BATCH * SEQ // P, DM])
        attn = sb("attn", [P, ITERS, BATCH, TPC, 2 * HG * DH])
        vop = sb("vop", [P, BATCH, TB, NH, VW])
        kop = sb("kop", [P, BATCH, NH, SEQ], BF16)
        qop = sb("qop", [P, 4, HG, HALF], BF16)
        prob = sb("prob", [P, PSLOTS, HALF])
        acc_sb = sb("acc_sb", [P, 2, HALF])
        identf = sb("identf", [P, P])
        identb = sb("identb", [P, P], BF16)
        ones = sb("ones", [P, P])
        mx = sb("mx", [P, 2, PAIRS])
        mrest = sb("mrest", [P, PAIRS])
        mpc = sb("mpc", [P, 2, P], BF16)
        mrow = sb("mrow", [PIECES * PAIRS, 2, P], BF16)
        rden = sb("rden", [P, TPC, HG])
        w1 = sb("w1", [P, 4])
        wraw = sb("wraw", [P, 3, DM])
        WT = sb("WT", [P, KC, 3 * P])
        memd = sb("memd", [P, 130])
        pcs = [sb(f"pcs{j}", [P, PIECES, HALF], BF16) for j in range(3)]
        rest = [sb(f"rest{j}", [P, HALF]) for j in range(3)]
        elu_e = [sb(f"elu_e{j}", [P, HALF]) for j in range(2)]
        sig = [sb(f"sig{j}", [P, HALF]) for j in range(2)]
        amem = sb("amem", [P, 2, DM])
        rmem = sb("rmem", [P, 2, 4])
        xT = prob[:, 0:4, :].rearrange("p (k c) s -> p k c s", k=KC)
        fraw = sb("fraw", [P, ER * DM])
        tern = sb("tern", [P, 3, ER * DM], BF16)
        tneg = sb("tneg", [P, ER * DM], BF16)
        wsum = sb("wsum", [P, 3])
        wscale = sb("wscale", [P, 3, 3])
        upT = sb("upT", [P, 2, KC, DE], BF16)
        upT_fine = sb("upT_fine", [P, 2, KC, DE], BF16)
        downT = kop[:, 0, 0:4, :].rearrange("p h s -> p (h s)").bitcast(F32).rearrange("p (r d) -> p r d", r=ER)
        yout = kop[:, 0, 4:8, :].rearrange("p h s -> p (h s)").bitcast(F32).rearrange("p (b t d) -> p b t d", b=2, t=TPC)
        z = kop[:, 1, 0:4, :].rearrange("p h s -> p (h s)").bitcast(F32).rearrange("p (b t d) -> p b t d", b=2, t=TPC)
        zp = kop[:, 1, 4:8, :].rearrange("p h s -> p (h s)").bitcast(FP16).rearrange("p (b e k s) -> p b e k s", b=2, e=2, k=KC)
        hidden = prob
        silu = acc_sb
        stat = sb("stat", [P, TPC, 6])
        mv = sb("mv", [P, TPC, 2])
        spare = sb("spare", [P, 1])
        rstd = sb("rstd", [P, TPC])
        negexp = sb("negexp", [P, TPC])
        zeros = sb("zeros", [P, PAIRS])
        coarse = sb("coarse", [P, 1])
        zc = fraw[:, 0:KC * HALF].rearrange("p (k s) -> p k s", k=KC)

        ps = ctx.enter_context(nc.psum_tensor("ps", [P, 8, HALF], F32))
        ACC, MISC_SLOT, SEL0 = 7, 12, 64
        MISC = 4 + MISC_SLOT % 3

        def slot_of(t):
            return t + (t >= MISC_SLOT)


        qd = nc.dram_tensor("q_pieces", (PIECES, BATCH, ITERS, DKV, HALF), BF16, kind="Internal").ap()
        kd = nc.dram_tensor("k_pieces", (PIECES, BATCH, DKV, SEQ), BF16, kind="Internal").ap()

        x_in = [sem(f"x_in{c}") for c in range(CHUNKS)]
        zero_rows = sem("zero_rows")
        memd_zero, w_in, mem_in, mw_in = sem("memd_zero"), sem("w_in"), sem("mem_in"), sem("mw_in")
        ident_ready, const_ready = sem("ident_ready"), sem("const_ready")
        wt_ready, wt_copied = sem("wt_ready"), sem("wt_copied")
        xt_ready, xt_copied = sem("xt_ready"), sem("xt_copied")
        proj_ready, hi_done, v_done = sem("proj_ready"), sem("hi_done"), sem("v_done")
        rest_done, mid_done, lo_done = sem("rest_done"), sem("mid_done"), sem("lo_done")
        neg_done, exp_done, em_done, sig_done = sem("neg_done"), sem("exp_done"), sem("em_done"), sem("sig_done")
        pc_out = [sem(f"pc_out{j}") for j in range(3)]
        mem_ready, mem_scaled, xr_done = sem("mem_ready"), sem("mem_scaled"), sem("xr_done")
        w_step, rm_step = sem("w_step"), sem("rm_step")
        kop_in = [sem(f"kop_in{b}") for b in range(BATCH)]
        qop_in = [sem(f"qop_in{c}") for c in range(4)]
        mrow_in = [sem(f"mrow_in{c}") for c in range(4)]
        score_a, max_done = sem("score_a"), sem("max_done")
        split_step, mt_ready, mt_copied = sem("split_step"), sem("mt_ready"), sem("mt_copied")
        score_b, prob_done, pv_done = sem("score_b"), sem("prob_done"), sem("pv_done")
        acc_saved, sel_ready, rden_done, sel_used = sem("acc_saved"), sem("sel_ready"), sem("rden_done"), sem("sel_used")
        f_in, fsum_done, fsum_all, fscale_step = sem("f_in"), sem("fsum_done"), sem("fsum_all"), sem("fscale_step")
        f_in2, tern_step = sem("f_in2"), sem("tern_step")
        tt_ready, tt_dve, tt_act = sem("tt_ready"), sem("tt_dve"), sem("tt_act")
        y_done, stat_done, var_done, rstd_done = sem("y_done"), sem("stat_done"), sem("var_done"), sem("rstd_done")
        z_done, zt_ready, zhi_done, zrest_done, zp_done = sem("z_done"), sem("zt_ready"), sem("zhi_done"), sem("zrest_done"), sem("zp_done")
        up_ready, gate_ready, silu_done, hid_done = sem("up_ready"), sem("gate_ready"), sem("silu_done"), sem("hid_done")
        down_ready, y2_done, yout_done = sem("down_ready"), sem("y2_done"), sem("yout_done")
        out_done = [sem(f"out_done{b}") for b in range(BATCH)]

        x_t = x.rearrange("b (t p) d -> p (b t) d", p=P)
        out_t = out.rearrange("b (t p) d -> p (b t) d", p=P)
        f_dram = [W_up.rearrange("(p r) d -> p (r d)", r=ER), W_gate.rearrange("(p r) d -> p (r d)", r=ER),
                  W_down.rearrange("(c p) e -> p c e", p=P)]

        def fraw_to(w):
            return fraw[:, :].rearrange("p (c e) -> p c e", c=KC) if w == 2 else fraw[:, :]

        def at(i, c, k):
            return i + (c + k) // 4, (c + k) % 4

        def is_first(i, c):
            return isinstance(i, int) and 4 * i + c == 0

        def exists(i, c, k):
            return not isinstance(i, int) or 4 * i + c + k < QUADS

        def all_quads(eng, quad):
            for c in range(4):
                quad(0, c)
            with eng.Fori(1, ITERS - 1) as i:
                for c in range(4):
                    quad(i, c)
            for c in range(4):
                quad(ITERS - 1, c)

        block = ctx.enter_context(nc.Block())

        @block.sync
        def _(sp):
            sp.dma_start(wraw[:, 0:2, :], Wq.rearrange("(c p) d -> p c d", p=P)).then_inc(w_in, 16)
            sp.dma_start(wraw[0:DKV, 2, :], Wk).then_inc(w_in, 16)
            sp.dma_start(wraw[DKV:P, 2, :], Wv).then_inc(w_in, 16)
            for ch in range(CHUNKS):
                sp.dma_start(xr[:, TPC * ch:TPC * (ch + 1), :], x_t[:, TPC * ch:TPC * (ch + 1), :]).then_inc(x_in[ch], 16)

            sp.wait_ge(memd_zero, 1)
            for k in range(2):
                sp.dma_start(memd[DKV * k:DKV * (k + 1), DKV * k:DKV * (k + 1)], memory).then_inc(mem_in, 16)
                sp.dma_start(memd[DKV * k:DKV * (k + 1), P + k:P + k + 1], memory_norm).then_inc(mem_in, 16)
            sp.dma_start(w1[:, 0:1], memory_weight.rearrange("(o n) -> o n", o=1).broadcast_to([P, 1])).then_inc(mw_in, 16)

            def load_qop(i, c):
                b, hg = c // 2, c % 2
                for a in range(PIECES):
                    src = qd[a, b, i, hg * HG * DH:(hg + 1) * HG * DH, :].rearrange("(h d) s -> d h s", d=DH)
                    for k in range(PIECES):
                        r = DH * (PIECES * a + k)
                        sp.dma_start(qop[r:r + DH, c, :, :], src).then_inc(qop_in[c], 16)

            for ch in range(CHUNKS):
                b, hs = ch // 2, ch % 2
                for j in range(3):
                    sp.wait_ge(lo_done, 3 * ch + j + 1)
                    if j < 2:
                        dst = qd[:, b, hs * NQ + 2 * j:hs * NQ + 2 * j + 2].rearrange("a n f s -> (n f) a s")
                        sp.dma_start(dst, pcs[j][:, :, :]).then_inc(pc_out[j], 16)
                    else:
                        dst = kd[:, b, :, hs * HALF:(hs + 1) * HALF].rearrange("a f s -> f a s")
                        sp.dma_start(dst, pcs[2][0:DKV, :, :]).then_inc(pc_out[j], 16)
                if ch == 0:
                    sp.wait_ge(zero_rows, 2)
                    sp.wait_ge(pc_out[0], 16)
                    load_qop(0, 0)
                    load_qop(0, 1)
                if ch == 2:
                    sp.wait_ge(pc_out[0], 16 * 3)
                    load_qop(0, 2)
                if hs == 1:
                    sp.wait_ge(pc_out[2], 16 * (ch + 1))
                    for k in range(PIECES):
                        src = kd[k, b].rearrange("(h d) t -> d h t", d=DH)
                        for a in range(PIECES):
                            r = DH * (PIECES * a + k)
                            sp.dma_start(kop[r:r + DH, b, :, :], src).then_inc(kop_in[b], 16)
            for j in range(2):
                sp.wait_ge(pc_out[j], 16 * CHUNKS)

            def move_max(i, c):
                sp.wait_ge(mt_copied, 4 * i + c + 1)
                for a in range(PIECES):
                    sp.dma_start(qop[MAX_ROW + a:MAX_ROW + a + 1, c, :, :].rearrange("o h s -> o (h s)"),
                                 mrow[PAIRS * a:PAIRS * (a + 1), c % 2, :]).then_inc(mrow_in[c], 16)

            def quad(i, c):
                if exists(i, c, 3):
                    sp.wait_ge(score_b, TILES * (4 * i + c))
                    load_qop(*at(i, c, 3))
                if exists(i, c, 1):
                    move_max(*at(i, c, 1))

            move_max(0, 0)
            all_quads(sp, quad)

            with sp.Fori(0, SEQ // HALF) as hs:
                for b in range(BATCH):
                    sp.wait_ge(yout_done, TPC * (2 * hs + b + 1))
                    sp.dma_start(out_t[:, bass.ds(TB * b + TPC * hs, TPC), :], yout[:, b, :, :]).then_inc(out_done[b], 16)
            for b in range(BATCH):
                sp.wait_ge(out_done[b], 16 * (SEQ // HALF))

        @block.gpsimd
        def _(pool):
            pool.memset(identf[:, :], 0.0).then_inc(ident_ready, 1)
            pool.wait_ge(ident_ready, 1)
            pool.affine_select(out=identf[:, :], in_=identf[:, :], compare_op=ALU.not_equal, fill=1.0,
                               base=0, pattern=[[-1, P]], channel_multiplier=1).then_inc(ident_ready, 1)
            pool.wait_ge(ident_ready, 2)
            pool.memset(memd[:, :], 0.0).then_inc(memd_zero, 1)
            pool.tensor_copy(identb[:, :], identf[:, :]).then_inc(const_ready, 1)
            pool.memset(vop[:, :, :, :, :], 0.0).then_inc(const_ready, 1)
            pool.wait_ge(const_ready, 2)
            pool.memset(vop[:, :, :, :, DH:DH + 1], 1.0).then_inc(const_ready, 1)
            pool.memset(ones[:, :], 1.0).then_inc(const_ready, 1)
            pool.memset(negexp[:, :], -0.5).then_inc(const_ready, 1)
            pool.memset(mpc[:, :, :], 0.0).then_inc(const_ready, 1)
            pool.memset(zeros[:, :], 0.0).then_inc(const_ready, 1)
            pool.memset(coarse[:, :], 1.0 / FINE).then_inc(const_ready, 1)
            pool.wait_ge(const_ready, CONSTS - 1)
            pool.memset(kop[MAX_ROW:ROWS, :, :, :], 1.0).then_inc(const_ready, 1)
            pool.wait_ge(const_ready, CONSTS)

            def add_mem(ch):
                for st in range(TPC):
                    n = TPC * ch + st
                    pool.wait_ge(mem_scaled, n + 1)
                    pool.tensor_tensor(xr[:, n, :], xr[:, n, :], amem[:, n % 2, :], ALU.add).then_inc(xr_done, 1)

            for ch in range(CHUNKS):
                for j in range(3):
                    np_ = P if j < 2 else DKV
                    pool.wait_ge(mid_done, 3 * ch + j + 1)
                    pool.tensor_tensor(pcs[j][0:np_, 2, :], rest[j][0:np_, :], pcs[j][0:np_, 1, :], ALU.subtract).then_inc(lo_done, 1)
                for j in range(2):
                    pool.wait_ge(exp_done, 2 * ch + j + 1)
                    pool.tensor_scalar(elu_e[j][:, :], elu_e[j][:, :], -1.0, None, ALU.add).then_inc(em_done, 1)
                if ch:
                    add_mem(ch - 1)
            add_mem(CHUNKS - 1)

            def split_max(i, c):
                q = 4 * i + c
                if not (isinstance(i, int) and q < 2):
                    pool.wait_ge(mt_ready, q - 1)
                pool.wait_ge(max_done, PAIRS * (q + 1))
                m, pc = mx[:, c % 2, :], mpc[:, c % 2, :]
                pool.tensor_tensor(pc[:, 0:PAIRS], m, zeros[:, :], ALU.add).then_inc(split_step, 1)
                pool.wait_ge(split_step, 4 * q + 1)
                pool.tensor_tensor(mrest[:, :], m, pc[:, 0:PAIRS], ALU.subtract).then_inc(split_step, 1)
                pool.wait_ge(split_step, 4 * q + 2)
                pool.tensor_tensor(pc[:, PAIRS:2 * PAIRS], mrest[:, :], zeros[:, :], ALU.add).then_inc(split_step, 1)
                pool.wait_ge(split_step, 4 * q + 3)
                pool.tensor_tensor(pc[:, 2 * PAIRS:3 * PAIRS], mrest[:, :], pc[:, PAIRS:2 * PAIRS], ALU.subtract).then_inc(split_step, 1)

            def ternary(w):
                pool.wait_ge(f_in2, 16 * (w + 1))
                raw = fraw[:, :]
                pool.tensor_scalar(tneg[:, :], raw, wscale[:, w, 2:3], None, ALU.is_lt).then_inc(tern_step, 1)
                pool.tensor_scalar(tern[:, w, :], raw, wscale[:, w, 1:2], None, ALU.is_gt).then_inc(tern_step, 1)
                pool.wait_ge(tern_step, 3 * w + 2)
                pool.tensor_tensor(tern[:, w, :], tern[:, w, :], tneg[:, :], ALU.subtract).then_inc(tern_step, 1)
                pool.wait_ge(tern_step, 3 * w + 3)

            def quad(i, c):
                if exists(i, c, 1):
                    split_max(*at(i, c, 1))
                if isinstance(i, int) and i == 0 and c > 0:
                    if c == 1:
                        pool.wait_ge(fscale_step, 3)
                    ternary(c - 1)

            split_max(0, 0)
            all_quads(pool, quad)

            def rsqrt(n):
                pool.wait_ge(var_done, n + 1)
                pool.tensor_tensor(rstd[:, :], rstd[:, :], negexp[:, 0:TPC], ALU.pow).then_inc(rstd_done, 1)

            def low_pieces(g, b):
                for kc in range(KC):
                    pool.wait_ge(zrest_done, KC * g + kc + 1)
                    pool.tensor_tensor(zp[:, b, 1, kc, :], zc[:, kc, :], coarse[:, :].broadcast_to([P, HALF]), ALU.mult).then_inc(zp_done, 1)

            with pool.Fori(0, SEQ // HALF) as hs:
                rsqrt(4 * hs)
                low_pieces(2 * hs, 0)
                rsqrt(4 * hs + 1)
                low_pieces(2 * hs + 1, 1)
                rsqrt(4 * hs + 2)
                rsqrt(4 * hs + 3)

        @block.scalar
        def _(act):
            act.dma_start(fraw_to(0), f_dram[0]).then_inc(f_in, 16)
            for kc in range(KC):
                act.wait_ge(wt_ready, kc + 1)
                nc.scalar.activation(WT[:, kc, :], ps[:, kc, 0:3 * P], ACT.Copy).then_inc(wt_copied, 1)

            for ch in range(CHUNKS):
                b, hs = ch // 2, ch % 2
                for kc in range(KC):
                    act.wait_ge(xt_ready, KC * ch + kc + 1)
                    if ch >= 2:
                        act.wait_ge(proj_ready, 4 * (ch - 1))
                    nc.scalar.activation(xT[:, kc, ch % 2, :], ps[:, kc, :], ACT.Copy).then_inc(xt_copied, 1)
                for j in range(3):
                    np_ = P if j < 2 else DKV
                    act.wait_ge(proj_ready, 4 * ch + j + 1)
                    if ch:
                        act.wait_ge(pc_out[j], 16 * ch)
                    nc.scalar.activation(pcs[j][0:np_, 0, :], ps[0:np_, 2 + j, :], ACT.Copy).then_inc(hi_done, 1)
                for j in range(3):
                    np_ = P if j < 2 else DKV
                    act.wait_ge(rest_done, 3 * ch + j + 1)
                    nc.scalar.activation(pcs[j][0:np_, 1, :], rest[j][0:np_, :], ACT.Copy).then_inc(mid_done, 1)
                    if j < 2:
                        if ch:
                            act.wait_ge(sig_done, 2 * (ch - 1) + j + 1)
                        nc.scalar.activation(elu_e[j][:, :], ps[:, 2 + j, :], ACT.Relu, scale=-1.0).then_inc(neg_done, 1)
                act.wait_ge(proj_ready, 4 * ch + 4)
                act.wait_ge(const_ready, CONSTS)
                nc.scalar.activation(vop[:, b, hs * TPC:(hs + 1) * TPC, :, 0:DH],
                                     ps[:, 5, 0:TPC * DKV].rearrange("p (t h d) -> p t h d", t=TPC, h=NH),
                                     ACT.Copy).then_inc(v_done, 1)
                for j in range(2):
                    act.wait_ge(neg_done, 2 * ch + j + 1)
                    nc.scalar.activation(elu_e[j][:, :], elu_e[j][:, :], ACT.Exp, scale=-1.0).then_inc(exp_done, 1)
                if ch == 0:
                    act.wait_ge(mw_in, 16)
                    nc.scalar.activation(w1[:, 1:2], w1[:, 0:1], ACT.Exp, scale=-1.0).then_inc(w_step, 1)
            for w in range(3):
                act.wait_ge(f_in, 16 * (w + 1))
                nc.scalar.activation(tern[:, w, :], fraw[:, :], ACT.Abs, accum_out=wsum[:, w:w + 1]).then_inc(fsum_done, 1)
                act.wait_ge(fsum_done, w + 1)
                if w < 2:
                    act.dma_start(fraw_to(w + 1), f_dram[w + 1]).then_inc(f_in, 16)
            act.dma_start(fraw_to(0), f_dram[0]).then_inc(f_in2, 16)

            def save_acc(i, c):
                q = 4 * i + c
                act.wait_ge(pv_done, TILES * (q + 1))
                if not (isinstance(i, int) and q < 2):
                    act.wait_ge(sel_ready, q - 1)
                nc.scalar.activation(acc_sb[:, c % 2, :], ps[:, ACC, :], ACT.Copy).then_inc(acc_saved, 1)

            def quad(i, c):
                q = 4 * i + c
                first = isinstance(i, int) and q == 0
                for t in range(TILES):
                    act.wait_ge(score_b, TILES * q + t + 1)
                    if not (first and t < PSLOTS):
                        act.wait_ge(pv_done, TILES * q + t + 1 - PSLOTS)
                    nc.scalar.activation(prob[:, t % PSLOTS, :], ps[:, 4 + slot_of(t) % 3, :], ACT.Exp,
                                         scale=SCALE).then_inc(prob_done, 1)
                    if t == HG - 1 and not first:
                        save_acc(*at(i, c, -1))
                if isinstance(i, int) and i == 0 and c in (1, 2):
                    act.wait_ge(tern_step, 3 * c)
                    act.dma_start(fraw_to(c), f_dram[c]).then_inc(f_in2, 16)

            all_quads(act, quad)
            save_acc(ITERS - 1, 3)

            for k in range(6):
                act.wait_ge(tt_ready, k + 1)
                dst = upT[:, k // 2, k % 2, :] if k < 4 else downT[:, 4 * (k - 4):4 * (k - 3), :].rearrange("p r d -> p (r d)")
                nc.scalar.activation(dst, ps[:, k, :].bitcast(BF16), ACT.Copy).then_inc(tt_act, 1)

            with act.Fori(0, SEQ // HALF) as hs:
                for b in range(BATCH):
                    g = 2 * hs + b
                    for kc in range(KC):
                        act.wait_ge(zt_ready, KC * g + kc + 1)
                        nc.scalar.activation(zp[:, b, 0, kc, :], ps[:, 4 + kc, :], ACT.Copy).then_inc(zhi_done, 1)
                    for r in range(ER):
                        act.wait_ge(up_ready, ER * g + r + 1)
                        act.wait_ge(hid_done, ER * g + max(r - 1, 0))
                        nc.scalar.activation(silu[:, r % 2, :], ps[:, r % 2, :], ACT.Silu,
                                             scale=wscale[:, 0, 0:1]).then_inc(silu_done, 1)

        @block.vector
        def _(dve):
            v = nc.vector
            v.memset(qop[64:MAX_ROW, :, :, :].rearrange("r c h s -> r (c h s)").bitcast(F32), 0.0).then_inc(zero_rows, 1)
            v.memset(kop[64:MAX_ROW, :, :, :].rearrange("r b h s -> r (b h s)").bitcast(F32), 0.0).then_inc(zero_rows, 1)
            def memory_weight_sigmoid():
                dve.wait_ge(w_step, 1)
                v.tensor_scalar(w1[:, 1:2], w1[:, 1:2], 1.0, None, ALU.add).then_inc(w_step, 1)
                dve.wait_ge(w_step, 2)
                v.reciprocal(w1[:, 2:3], w1[:, 1:2]).then_inc(w_step, 1)
                dve.wait_ge(w_step, 3)
                v.tensor_scalar(w1[:, 3:4], w1[:, 2:3], -1.0, 1.0, ALU.mult, ALU.add).then_inc(w_step, 1)

            def scale_mem(ch):
                for st in range(TPC):
                    n = TPC * ch + st
                    num = ps[:, 6 + n % 2, 0:260].rearrange("p (f c) -> p f c", f=2)
                    dve.wait_ge(mem_ready, n + 1)
                    rm = rmem[:, n % 2, :].rearrange("p (f m) -> p f m", f=2)
                    v.reciprocal(rm, num[:, :, P:P + 2]).then_inc(rm_step, 1)
                    dve.wait_ge(rm_step, 2 * n + 1)
                    v.tensor_scalar(rmem[:, n % 2, :], rmem[:, n % 2, :], w1[:, 2:3], None, ALU.mult).then_inc(rm_step, 1)
                    dve.wait_ge(rm_step, 2 * n + 2)
                    if n >= 2:
                        dve.wait_ge(xr_done, n - 1)
                    v.tensor_tensor(amem[:, n % 2, :].rearrange("p (f m k) -> p f m k", f=2, m=2),
                                    num[:, :, 0:P].rearrange("p f (m k) -> p f m k", m=2),
                                    rm.unsqueeze(3).broadcast_to([P, 2, 2, DKV]), ALU.mult).then_inc(mem_scaled, 1)

            for ch in range(CHUNKS):
                for j in range(3):
                    np_ = P if j < 2 else DKV
                    dve.wait_ge(hi_done, 3 * ch + j + 1)
                    if ch:
                        dve.wait_ge(lo_done, 3 * (ch - 1) + j + 1)
                    v.tensor_tensor(rest[j][0:np_, :], ps[0:np_, 2 + j, :], pcs[j][0:np_, 0, :], ALU.subtract).then_inc(rest_done, 1)
                if ch == 1:
                    memory_weight_sigmoid()
                if ch:
                    scale_mem(ch - 1)
                for j in range(2):
                    dve.wait_ge(em_done, 2 * ch + j + 1)
                    v.scalar_tensor_tensor(out=sig[j][:, :], in0=ps[:, 2 + j, :], scalar=0.0, in1=elu_e[j][:, :],
                                           op0=ALU.max, op1=ALU.add).then_inc(sig_done, 1)
            scale_mem(CHUNKS - 1)

            def take_max(i, c, pairs):
                q = 4 * i + c
                for p in pairs:
                    dve.wait_ge(score_a, PAIRS * q + p + 1)
                    if p == 0 and not (isinstance(i, int) and q < 2):
                        dve.wait_ge(split_step, 4 * (q - 1))
                    v.tensor_reduce(mx[:, c % 2, p:p + 1], ps[:, 2 * (p % 2):2 * (p % 2) + 2, :],
                                    AX.XY, ALU.max, negate=True).then_inc(max_done, 1)

            def copy_mt(i, c):
                q = 4 * i + c
                dve.wait_ge(mt_ready, q + 1)
                if not (isinstance(i, int) and q < 2):
                    if isinstance(i, int) and i == 0:
                        dve.wait_ge(mrow_in[(c - 2) % 4], 16 * PIECES)
                    elif c >= 2:
                        dve.wait_ge(mrow_in[c - 2], 16 * PIECES * (i + 1))
                    else:
                        dve.wait_ge(mrow_in[c + 2], 16 * PIECES * i)
                v.tensor_copy(mrow[:, c % 2, :], ps[0:PIECES * PAIRS, MISC, 0:P // 2].bitcast(BF16)).then_inc(mt_copied, 1)

            def normalize(i, c):
                q = 4 * i + c
                sel = ps[:, MISC, SEL0:SEL0 + TPC * HG * 9].rearrange("p (t h w) -> p t h w", t=TPC, h=HG)
                dve.wait_ge(sel_ready, q + 1)
                v.reciprocal(rden[:, :, :], sel[:, :, :, DH]).then_inc(rden_done, 1)
                dve.wait_ge(rden_done, q + 1)
                v.tensor_tensor(attn[:, i, c // 2, :, HG * DH * (c % 2):HG * DH * (c % 2 + 1)].rearrange("p t (h d) -> p t h d", h=HG),
                                sel[:, :, :, 0:DH], rden[:, :, :].unsqueeze(3).broadcast_to([P, TPC, HG, DH]),
                                ALU.mult).then_inc(sel_used, 1)

            def quad(i, c):
                has_max = exists(i, c, 2)
                if has_max:
                    take_max(*at(i, c, 2), range(0, 6))
                if exists(i, c, 1):
                    copy_mt(*at(i, c, 1))
                if not is_first(i, c):
                    normalize(*at(i, c, -1))
                if has_max:
                    take_max(*at(i, c, 2), range(6, PAIRS))

            take_max(0, 0, range(PAIRS))
            take_max(0, 1, range(0, 4))
            copy_mt(0, 0)
            take_max(0, 1, range(4, PAIRS))
            dve.wait_ge(fsum_all, 1)
            v.tensor_scalar(wscale[:, :, 0], ps[:, MISC, 0:3], 1.0 / (DE * DM), Q_EPS, ALU.mult, ALU.add).then_inc(fscale_step, 1)
            dve.wait_ge(fscale_step, 1)
            v.tensor_scalar(wscale[:, :, 1], wscale[:, :, 0], 0.5, None, ALU.mult).then_inc(fscale_step, 1)
            v.tensor_scalar(wscale[:, :, 2], wscale[:, :, 0], -0.5, None, ALU.mult).then_inc(fscale_step, 1)
            all_quads(dve, quad)
            normalize(ITERS - 1, 3)

            for k in range(4):
                dve.wait_ge(tt_act, k + 1)
                v.tensor_scalar(upT_fine[:, k // 2, k % 2, :], upT[:, k // 2, k % 2, :], FINE, None, ALU.mult).then_inc(tt_dve, 1)

            def residual(g, hs, b):
                for st in range(TPC):
                    v.scalar_tensor_tensor(
                        out=z[:, b, st, :].rearrange("p (n k) -> p n k", n=NQ),
                        in0=attn[:, bass.ds(NQ * hs, NQ), b, st, :], scalar=w1[:, 3:4],
                        in1=xr[:, bass.ds(TB * b + TPC * hs + st, 1), :].rearrange("p o (n k) -> p (o n) k", n=NQ),
                        op0=ALU.mult, op1=ALU.add).then_inc(y_done, 1)
                dve.wait_ge(y_done, TPC * (g + 1))

            def layer_norm(n, b, dst, done):
                for st in range(TPC):
                    v.bn_stats(stat[:, st, :], z[:, b, st, :]).then_inc(stat_done, 1)
                dve.wait_ge(stat_done, 8 * n + 4)
                v.memset(spare[:, :], 0.0)
                for st in range(TPC):
                    v.bn_aggr(mv[:, st, :], stat[:, st, :]).then_inc(stat_done, 1)
                dve.wait_ge(stat_done, 8 * n + 8)
                v.tensor_scalar(rstd[:, :], mv[:, :, 1], LN_EPS, None, ALU.add).then_inc(var_done, 1)
                dve.wait_ge(rstd_done, n + 1)
                for st in range(TPC):
                    v.tensor_scalar(dst[:, st, :], z[:, b, st, :], mv[:, st, 0:1], rstd[:, st:st + 1],
                                    ALU.subtract, ALU.mult).then_inc(done, 1)

            def rest_pieces(g, b):
                for kc in range(KC):
                    dve.wait_ge(zhi_done, KC * g + kc + 1)
                    dve.wait_ge(zp_done, KC * g)
                    v.tensor_tensor(zc[:, kc, :], ps[:, 4 + kc, :], zp[:, b, 0, kc, :], ALU.subtract).then_inc(zrest_done, 1)

            def make_hidden(g, b):
                for r in range(ER):
                    dve.wait_ge(gate_ready, ER * g + r + 1)
                    dve.wait_ge(silu_done, ER * g + r + 1)
                    v.scalar_tensor_tensor(out=hidden[:, ER * b + r, :], in0=ps[:, 2 + r % 2, :], scalar=wscale[:, 1, 0:1],
                                           in1=silu[:, r % 2, :], op0=ALU.mult, op1=ALU.mult).then_inc(hid_done, 1)

            def add_down(g, b):
                for h in range(2):
                    dve.wait_ge(down_ready, 2 * g + h + 1)
                    zh = z[:, b, 2 * h:2 * h + 2, :]
                    v.scalar_tensor_tensor(out=zh, in0=ps[:, 6 + h, :].rearrange("p (t d) -> p t d", t=2),
                                           scalar=wscale[:, 2, 0:1], in1=zh,
                                           op0=ALU.mult, op1=ALU.add).then_inc(y2_done, 1)

            with dve.Fori(0, SEQ // HALF) as hs:
                g = 2 * hs
                residual(g, hs, 0)
                layer_norm(4 * hs, 0, z[:, 0, :, :], z_done)
                rest_pieces(g, 0)
                residual(g + 1, hs, 1)
                layer_norm(4 * hs + 1, 1, z[:, 1, :, :], z_done)
                make_hidden(g, 0)
                rest_pieces(g + 1, 1)
                add_down(g, 0)
                make_hidden(g + 1, 1)
                dve.wait_ge(y2_done, 2 * (g + 1))
                dve.wait_ge(out_done[0], 16 * hs)
                layer_norm(4 * hs + 2, 0, yout[:, 0, :, :], yout_done)
                add_down(g + 1, 1)
                dve.wait_ge(y2_done, 2 * (g + 2))
                dve.wait_ge(out_done[1], 16 * hs)
                layer_norm(4 * hs + 3, 1, yout[:, 1, :, :], yout_done)

        @block.tensor
        def _(pe):
            pe.wait_ge(ident_ready, 2)
            pe.wait_ge(w_in, 48)
            for kc in range(KC):
                for f in range(3):
                    last = pe.transpose(ps[:, kc, P * f:P * (f + 1)], wraw[:, f, P * kc:P * (kc + 1)], identf[:, :])
                last.then_inc(wt_ready, 1)

            def read_memory(ch):
                pe.wait_ge(mem_in, 64)
                pe.wait_ge(sig_done, 2 * ch + 2)
                for st in range(TPC):
                    n = TPC * ch + st
                    if n >= 2:
                        pe.wait_ge(mem_scaled, n - 1)
                    for f in range(2):
                        last = pe.matmul(ps[:, 6 + n % 2, 130 * f:130 * (f + 1)], sig[f][:, P * st:P * (st + 1)],
                                         memd[:, :], start=True, stop=True)
                    last.then_inc(mem_ready, 1)

            for ch in range(CHUNKS):
                pe.wait_ge(x_in[ch], 16)
                for kc in range(KC):
                    if ch == 0:
                        pe.wait_ge(wt_copied, kc + 1)
                    else:
                        pe.wait_ge(xt_copied, KC * (ch - 1) + kc + 1)
                    for st in range(TPC):
                        last = pe.transpose(ps[:, kc, P * st:P * (st + 1)], xr[:, TPC * ch + st, P * kc:P * (kc + 1)], identf[:, :])
                    last.then_inc(xt_ready, 1)
                pe.wait_ge(xt_copied, KC * (ch + 1))
                for j in range(3):
                    np_ = P if j < 2 else DKV
                    if ch and j < 2:
                        pe.wait_ge(sig_done, 2 * (ch - 1) + j + 1)
                    elif ch:
                        pe.wait_ge(rest_done, 3 * ch)
                    for kc in range(KC):
                        last = pe.matmul(ps[0:np_, 2 + j, :], WT[:, kc, P * j:P * j + np_], xT[:, kc, ch % 2, :],
                                         start=(kc == 0), stop=(kc == KC - 1))
                    last.then_inc(proj_ready, 1)
                if ch:
                    pe.wait_ge(v_done, ch)
                for st in range(TPC):
                    for kc in range(KC):
                        last = pe.matmul(ps[:, 5, DKV * st:DKV * (st + 1)], xT[:, kc, ch % 2, P * st:P * (st + 1)],
                                         WT[:, kc, 2 * P + DKV:3 * P], start=(kc == 0), stop=(kc == KC - 1))
                last.then_inc(proj_ready, 1)
                if ch:
                    read_memory(ch - 1)
            read_memory(CHUNKS - 1)

            def max_scores(i, c, pairs):
                q, b, hg = 4 * i + c, c // 2, c % 2
                for p in pairs:
                    j, st = p // TPC, p % TPC
                    if p == 0:
                        pe.wait_ge(qop_in[c], 16 * PIECES * PIECES * (i + 1))
                    if not (is_first(i, c) and p < 2):
                        pe.wait_ge(max_done, PAIRS * q + p - 1)
                    for half in range(2):
                        last = pe.matmul(ps[:, 2 * (p % 2) + half, :], qop[0:MAX_ROW, c, j, P * st:P * (st + 1)],
                                         kop[0:MAX_ROW, b, HG * hg + j, HALF * half:HALF * (half + 1)], start=True, stop=True)
                    last.then_inc(score_a, 1)

            def turn_max(i, c):
                q = 4 * i + c
                pe.wait_ge(split_step, 4 * (q + 1))
                pe.transpose(ps[:, MISC, 0:P // 2].bitcast(BF16), mpc[:, c % 2, :], identb[:, :]).then_inc(mt_ready, 1)

            def misc_read(i, c):
                if exists(i, c, 1):
                    pe.wait_ge(mt_copied, 4 * i + c + 2)
                if not is_first(i, c):
                    pe.wait_ge(sel_used, 4 * i + c)

            def scores(i, c, t):
                q, b, hg, tb, j = 4 * i + c, c // 2, c % 2, t // HG, t % HG
                if t == 0:
                    pe.wait_ge(mrow_in[c], 16 * PIECES * (i + 1))
                before = slot_of(t) - 3
                if before == MISC_SLOT:
                    misc_read(i, c)
                elif before >= 0 or not is_first(i, c):
                    pe.wait_ge(prob_done, TILES * q + before + 1 - (before > MISC_SLOT))
                pe.matmul(ps[:, 4 + slot_of(t) % 3, :], kop[0:ROWS, b, HG * hg + j, P * tb:P * (tb + 1)],
                          qop[0:ROWS, c, j, :], start=True, stop=True).then_inc(score_b, 1)

            def times_v(i, c, tb):
                q, b, hg = 4 * i + c, c // 2, c % 2
                if tb == 0:
                    pe.wait_ge(acc_saved, q)
                for j in range(HG):
                    t = HG * tb + j
                    pe.wait_ge(prob_done, TILES * q + t + 1)
                    pe.matmul(ps[VW * j:VW * (j + 1), ACC, :], vop[:, b, tb, HG * hg + j, :], prob[:, t % PSLOTS, :],
                              start=(tb == 0), stop=(tb == TB - 1)).then_inc(pv_done, 1)

            def select(i, c):
                q = 4 * i + c
                pe.wait_ge(acc_saved, q + 1)
                pick = identf[:, :].rearrange("p (h r) -> p h r", h=HG)[:, :, 0:DH + 1]
                for st in range(TPC):
                    last = pe.matmul(ps[:, MISC, SEL0 + 36 * st:SEL0 + 36 * (st + 1)], acc_sb[:, c % 2, P * st:P * (st + 1)], pick,
                                     start=True, stop=True)
                last.then_inc(sel_ready, 1)

            def quad(i, c):
                for tb in range(TB):
                    if HG * tb == MISC_SLOT:
                        pe.wait_ge(prob_done, TILES * (4 * i + c) + MISC_SLOT - 2)
                        if not is_first(i, c):
                            select(*at(i, c, -1))
                        if exists(i, c, 1):
                            turn_max(*at(i, c, 1))
                    scores(i, c, HG * tb)
                    if exists(i, c, 2):
                        max_scores(*at(i, c, 2), [2 * tb])
                    scores(i, c, HG * tb + 1)
                    scores(i, c, HG * tb + 2)
                    if exists(i, c, 2):
                        max_scores(*at(i, c, 2), [2 * tb + 1])
                    scores(i, c, HG * tb + 3)
                    if tb:
                        times_v(i, c, tb - 1)
                    elif not is_first(i, c):
                        times_v(*at(i, c, -1), TB - 1)

            pe.wait_ge(xt_copied, KC * CHUNKS)
            pe.wait_ge(sig_done, 2 * CHUNKS)
            pe.wait_ge(rest_done, 3 * CHUNKS)
            pe.wait_ge(v_done, CHUNKS)
            pe.wait_ge(mem_scaled, TPC * CHUNKS)
            pe.wait_ge(kop_in[0], 16 * PIECES * PIECES)
            pe.wait_ge(const_ready, CONSTS)
            max_scores(0, 0, range(PAIRS))
            max_scores(0, 1, range(0, 4))
            turn_max(0, 0)
            max_scores(0, 1, range(4, PAIRS))
            pe.wait_ge(fsum_done, 3)
            pe.wait_ge(mt_copied, 1)
            pe.matmul(ps[:, MISC, 0:3], ones[:, :], wsum[:, :], start=True, stop=True).then_inc(fsum_all, 1)
            pe.wait_ge(fscale_step, 1)
            pe.wait_ge(kop_in[1], 16 * PIECES * PIECES)
            all_quads(pe, quad)
            times_v(ITERS - 1, 3, TB - 1)
            pe.wait_ge(sel_used, QUADS - 1)
            pe.wait_ge(prob_done, TILES * QUADS)
            select(ITERS - 1, 3)

            pe.wait_ge(prob_done, TILES * QUADS)
            pe.wait_ge(tern_step, 9)
            for w in range(2):
                for kc in range(KC):
                    for r in range(ER):
                        last = pe.transpose(ps[:, KC * w + kc, :].bitcast(BF16)[:, P * r:P * (r + 1)],
                                            tern[:, w, DM * r + P * kc:DM * r + P * (kc + 1)], identb[:, :])
                    last.then_inc(tt_ready, 1)
            pe.wait_ge(sel_used, QUADS)
            tdown = tern[:, 2, :].rearrange("p (k e r) -> p k e r", k=KC, r=ER)
            for h in range(2):
                for r in range(4):
                    for kc in range(KC):
                        last = pe.transpose(ps[:, 4 + h, :].bitcast(BF16)[:, DM * r + P * kc:DM * r + P * (kc + 1)],
                                            tdown[:, kc, :, 4 * h + r], identb[:, :])
                last.then_inc(tt_ready, 1)
            pe.wait_ge(tt_act, 6)
            pe.wait_ge(tt_dve, 4)

            def turn_rows(g, b):
                pe.wait_ge(z_done, TPC * (g + 1))
                pe.wait_ge(zrest_done, KC * g)
                for kc in range(KC):
                    for st in range(TPC):
                        last = pe.transpose(ps[:, 4 + kc, P * st:P * (st + 1)], z[:, b, st, P * kc:P * (kc + 1)], identf[:, :])
                    last.then_inc(zt_ready, 1)

            def up_gate(g, b):
                pe.wait_ge(zp_done, KC * (g + 1))
                for r in range(ER):
                    pe.wait_ge(hid_done, ER * g + max(r - 1, 0))
                    for w, ready in ((0, up_ready), (1, gate_ready)):
                        for kc in range(KC):
                            for e, wt in ((0, upT), (1, upT_fine)):
                                last = pe.matmul(ps[:, 2 * w + r % 2, :], wt[:, w, kc, P * r:P * (r + 1)], zp[:, b, e, kc, :],
                                                 start=(kc == 0 and e == 0), stop=(kc == KC - 1 and e == 1))
                        last.then_inc(ready, 1)

            def down(g, b):
                pe.wait_ge(hid_done, ER * (g + 1))
                pe.wait_ge(y2_done, 2 * g)
                for st in range(TPC):
                    for r in range(ER):
                        last = pe.matmul(ps[:, 6 + st // 2, DM * (st % 2):DM * (st % 2 + 1)],
                                         hidden[:, ER * b + r, P * st:P * (st + 1)], downT[:, r, :],
                                         start=(r == 0), stop=(r == ER - 1))
                    if st % 2:
                        last.then_inc(down_ready, 1)

            with pe.Fori(0, SEQ // HALF) as hs:
                g = 2 * hs
                turn_rows(g, 0)
                up_gate(g, 0)
                turn_rows(g + 1, 1)
                down(g, 0)
                up_gate(g + 1, 1)
                down(g + 1, 1)


_INS = ["L0_attn_x", "L0_attn_Wq", "L0_attn_Wk", "L0_attn_Wv", "L0_attn_memory", "L0_attn_memory_norm",
        "L0_attn_memory_weight", "L0_ffn_W_up", "L0_ffn_W_gate", "L0_ffn_W_down"]


def kernel(**inputs):
    import numpy as _np
    import concourse.bacc as _bacc
    from concourse import mybir as _mybir
    from concourse.bass_utils import run_bass_kernel_spmd as _run

    nc = _bacc.Bacc("TRN2", target_bir_lowering=False, num_devices=1)
    arrays, args = {}, []
    for name in _INS:
        a = _np.ascontiguousarray(inputs[name])
        arrays[f"in_{name}"] = a
        args.append(nc.dram_tensor(f"in_{name}", a.shape, _mybir.dt.from_np(a.dtype), kind="ExternalInput").ap())
    args.append(nc.dram_tensor("out_0", (2, 1024, 256), _mybir.dt.float32, kind="ExternalOutput").ap())
    attention_ffn_kernel(nc, *args)
    r = _run(nc, [arrays], core_ids=[0])
    return r.results[0]["out_0"]
```

```python
from contextlib import ExitStack

import concourse.bass as bass
from concourse import mybir

F32 = mybir.dt.float32
BF16 = mybir.dt.bfloat16
FP16 = mybir.dt.float16
ALU = mybir.AluOpType
ACT = mybir.ActivationFunctionType
AX = mybir.AxisListType

P = 128
BATCH, SEQ, DM = 2, 1024, 256
NQ, NH, DH = 4, 8, 8
DKV = NH * DH
DE = 1024
SCALE = float(1.0 / (DH ** 0.5))
LN_EPS = 1e-5
Q_EPS = 1e-8
PIECES = 3
HALF = 512
CHUNKS = BATCH * SEQ // HALF
TPC = HALF // P
KC = DM // P
PROD_ROWS = PIECES * PIECES * DH
MAX_ROW = 96
ROWS = MAX_ROW + PIECES
TB = SEQ // P
HG = 4
ITERS = (SEQ // HALF) * NQ
QUADS = 4 * ITERS
TILES = TB * HG
PAIRS = HG * TPC
VW = 32
SELW = (HG - 1) * VW + VW // 2
PSLOTS = 16
ER = DE // P
CONSTS = 9
FINE = 2.0 ** -11
HID = 2.0 ** -8


def attention_ffn_kernel(nc, x, Wq, Wk, Wv, memory, memory_norm, memory_weight, W_up, W_gate, W_down, out):
    with ExitStack() as ctx:
        def sb(name, shape, dt=F32):
            return ctx.enter_context(nc.sbuf_tensor(name, shape, dt))

        def sem(name):
            return ctx.enter_context(nc.semaphore(name))

        xr = sb("xr", [P, BATCH * SEQ // P, DM])
        attn = sb("attn", [P, ITERS, BATCH, TPC, 2 * HG * DH])
        vop = sb("vop", [P, BATCH, TB, NH, VW])
        kop = sb("kop", [P, BATCH, NH, SEQ], BF16)
        qop = sb("qop", [P, 4, HG, HALF], BF16)
        prob = sb("prob", [P, PSLOTS, HALF])
        acc_sb = sb("acc_sb", [P, 2, HALF])
        identf = sb("identf", [P, P])
        identb = sb("identb", [P, P], BF16)
        ones = sb("ones", [P, P])
        mx = sb("mx", [P, 2, PAIRS])
        mrest = sb("mrest", [P, PAIRS])
        mpc = sb("mpc", [P, 2, P], BF16)
        mrow = sb("mrow", [PIECES * PAIRS, 2, P], BF16)
        rden = sb("rden", [P, TPC, HG])
        w1 = sb("w1", [P, 4])
        wraw = sb("wraw", [P, 3, DM])
        WT = sb("WT", [P, KC, 3 * P])
        memd = sb("memd", [P, 130])
        pcs = [sb(f"pcs{j}", [P, PIECES, HALF], BF16) for j in range(3)]
        rest = [sb(f"rest{j}", [P, HALF]) for j in range(3)]
        elu_e = [sb(f"elu_e{j}", [P, HALF]) for j in range(2)]
        sig = [sb(f"sig{j}", [P, HALF]) for j in range(2)]
        amem = sb("amem", [P, 2, DM])
        rmem = sb("rmem", [P, 2, 4])
        xT = prob[:, 0:4, :].rearrange("p (k c) s -> p k c s", k=KC)
        fraw = sb("fraw", [P, ER * DM])
        tern = sb("tern", [P, 3, ER * DM], BF16)
        tneg = sb("tneg", [P, ER * DM], BF16)
        wsum = sb("wsum", [P, 3])
        wscale = sb("wscale", [P, 3, 3])
        upT = sb("upT", [P, 2, KC, DE], BF16)
        upT_fine = sb("upT_fine", [P, 2, KC, DE], BF16)
        downT = kop[:, 0, 0:2, :].rearrange("p h s -> p (h s)").rearrange("p (r d) -> p r d", r=ER)
        downT_fine = kop[:, 0, 2:4, :].rearrange("p h s -> p (h s)").rearrange("p (r d) -> p r d", r=ER)
        zp = kop[:, 0, 4:8, :].rearrange("p h s -> p (h s)").bitcast(FP16).rearrange("p (b e k s) -> p b e k s", b=2, e=2, k=KC)
        yout = kop[:, 1, 0:4, :].rearrange("p h s -> p (h s)").bitcast(F32).rearrange("p (b t d) -> p b t d", b=2, t=TPC)
        hid = rest
        hp = prob[:, :, :].rearrange("p t s -> p (t s)").bitcast(FP16).rearrange("p (b e r s) -> p b e r s", b=2, e=2, r=ER)
        hscale = sb("hscale", [P, 4])
        silu = elu_e
        stat = sb("stat", [P, TPC, 6])
        mv = sb("mv", [P, TPC, 2])
        spare = sb("spare", [P, 1])
        rstd = sb("rstd", [P, TPC])
        negexp = sb("negexp", [P, TPC])
        zeros = sb("zeros", [P, PAIRS])
        coarse = sb("coarse", [P, 1])
        zc = fraw[:, 0:KC * HALF].rearrange("p (k s) -> p k s", k=KC)

        ps = ctx.enter_context(nc.psum_tensor("ps", [P, 8, HALF], F32))
        DOWN_BANKS = (6, 7)
        ACC, MISC_SLOT, SEL0 = 7, 20, 64
        MISC = 4 + MISC_SLOT % 3

        def x_bank(ch, kc):
            return kc if ch < 2 else 4 + kc

        def proj_bank(ch, j):
            return ((2, 3, 4, 5), (6, 7, 4, 5), (6, 7, 5, 4), (6, 7, 5, 4))[ch][j]

        def mem_bank(ch, st):
            return st % 2 if ch < 2 else 4 + st % 2

        def slot_of(t):
            return t + (t >= MISC_SLOT)


        qd = nc.dram_tensor("q_pieces", (PIECES, BATCH, ITERS, DKV, HALF), BF16, kind="Internal").ap()
        kd = nc.dram_tensor("k_pieces", (PIECES, BATCH, DKV, SEQ), BF16, kind="Internal").ap()

        x_in = [sem(f"x_in{c}") for c in range(CHUNKS)]
        zero_rows = sem("zero_rows")
        memd_zero, w_in, mem_in, mw_in = sem("memd_zero"), sem("w_in"), sem("mem_in"), sem("mw_in")
        ident_ready, const_ready = sem("ident_ready"), sem("const_ready")
        wt_ready, wt_copied = sem("wt_ready"), sem("wt_copied")
        xt_ready, xt_copied = sem("xt_ready"), sem("xt_copied")
        proj_ready, hi_done, v_done = sem("proj_ready"), sem("hi_done"), sem("v_done")
        rest_done, mid_done, lo_done = sem("rest_done"), sem("mid_done"), sem("lo_done")
        neg_done, exp_done, em_done, sig_done = sem("neg_done"), sem("exp_done"), sem("em_done"), sem("sig_done")
        pc_out = [sem(f"pc_out{j}") for j in range(3)]
        mem_ready, mem_scaled, xr_done = sem("mem_ready"), sem("mem_scaled"), sem("xr_done")
        w_step, rm_step = sem("w_step"), sem("rm_step")
        kop_in = [sem(f"kop_in{b}") for b in range(BATCH)]
        qop_in = [sem(f"qop_in{c}") for c in range(4)]
        mrow_in = [sem(f"mrow_in{c}") for c in range(4)]
        score_a, max_done = sem("score_a"), sem("max_done")
        split_step, mt_ready, mt_copied = sem("split_step"), sem("mt_ready"), sem("mt_copied")
        score_b, prob_done, pv_done = sem("score_b"), sem("prob_done"), sem("pv_done")
        acc_saved, sel_ready, rden_done, sel_used = sem("acc_saved"), sem("sel_ready"), sem("rden_done"), sem("sel_used")
        f_in, fsum_done, fsum_all, fscale_step = sem("f_in"), sem("fsum_done"), sem("fsum_all"), sem("fscale_step")
        f_in2, tern_step = sem("f_in2"), sem("tern_step")
        tt_ready, tt_copied, fine_done = sem("tt_ready"), sem("tt_copied"), sem("fine_done")
        y_done, stat_done, var_done, rstd_done = sem("y_done"), sem("stat_done"), sem("var_done"), sem("rstd_done")
        z_done, zt_ready, zhi_done, zrest_done, zp_done = sem("z_done"), sem("zt_ready"), sem("zhi_done"), sem("zrest_done"), sem("zp_done")
        up_ready, gate_ready, silu_done, hid_done = sem("up_ready"), sem("gate_ready"), sem("silu_done"), sem("hid_done")
        hhi_done, hrest_done, hlo_done = sem("hhi_done"), sem("hrest_done"), sem("hlo_done")
        down_ready, y2_done, yout_done = sem("down_ready"), sem("y2_done"), sem("yout_done")
        out_done = [sem(f"out_done{b}") for b in range(BATCH)]

        x_t = x.rearrange("b (t p) d -> p (b t) d", p=P)
        out_t = out.rearrange("b (t p) d -> p (b t) d", p=P)
        f_dram = [W_up.rearrange("(p r) d -> p (r d)", r=ER), W_gate.rearrange("(p r) d -> p (r d)", r=ER),
                  W_down.rearrange("(c p) e -> p c e", p=P)]

        def fraw_to(w):
            return fraw[:, :].rearrange("p (c e) -> p c e", c=KC) if w == 2 else fraw[:, :]

        def at(i, c, k):
            return i + (c + k) // 4, (c + k) % 4

        def is_last(i):
            return isinstance(i, int) and i == ITERS - 1

        def chunk(g):
            b, hs = g % 2, g // 2
            return b, hs, slice(TB * b + TPC * hs, TB * b + TPC * (hs + 1))

        def out_parts(g):
            return [slice(0, TPC)] if g + 1 < CHUNKS else [slice(0, 2), slice(2, TPC)]

        def zbank(g, kc):
            return (2 if g == 0 else 4) + kc

        def is_first(i, c):
            return isinstance(i, int) and 4 * i + c == 0

        def exists(i, c, k):
            return not isinstance(i, int) or 4 * i + c + k < QUADS

        def all_quads(eng, quad):
            for c in range(4):
                quad(0, c)
            with eng.Fori(1, ITERS - 1) as i:
                for c in range(4):
                    quad(i, c)
            for c in range(4):
                quad(ITERS - 1, c)

        block = ctx.enter_context(nc.Block())

        @block.sync
        def _(sp):
            sp.dma_start(wraw[:, 0:2, :], Wq.rearrange("(c p) d -> p c d", p=P)).then_inc(w_in, 16)
            sp.dma_start(wraw[0:DKV, 2, :], Wk).then_inc(w_in, 16)
            sp.dma_start(wraw[DKV:P, 2, :], Wv).then_inc(w_in, 16)
            for ch in range(CHUNKS):
                sp.dma_start(xr[:, TPC * ch:TPC * (ch + 1), :], x_t[:, TPC * ch:TPC * (ch + 1), :]).then_inc(x_in[ch], 16)

            sp.wait_ge(memd_zero, 1)
            for k in range(2):
                sp.dma_start(memd[DKV * k:DKV * (k + 1), DKV * k:DKV * (k + 1)], memory).then_inc(mem_in, 16)
                sp.dma_start(memd[DKV * k:DKV * (k + 1), P + k:P + k + 1], memory_norm).then_inc(mem_in, 16)
            sp.dma_start(w1[:, 0:1], memory_weight.rearrange("(o n) -> o n", o=1).broadcast_to([P, 1])).then_inc(mw_in, 16)

            def load_qop(i, c):
                b, hg = c // 2, c % 2
                for a in range(PIECES):
                    src = qd[a, b, i, hg * HG * DH:(hg + 1) * HG * DH, :].rearrange("(h d) s -> d h s", d=DH)
                    for k in range(PIECES):
                        r = DH * (PIECES * a + k)
                        sp.dma_start(qop[r:r + DH, c, :, :], src).then_inc(qop_in[c], 16)

            for ch in range(CHUNKS):
                b, hs = ch // 2, ch % 2
                for j in range(3):
                    sp.wait_ge(lo_done, 3 * ch + j + 1)
                    if j < 2:
                        dst = qd[:, b, hs * NQ + 2 * j:hs * NQ + 2 * j + 2].rearrange("a n f s -> (n f) a s")
                        sp.dma_start(dst, pcs[j][:, :, :]).then_inc(pc_out[j], 16)
                    else:
                        dst = kd[:, b, :, hs * HALF:(hs + 1) * HALF].rearrange("a f s -> f a s")
                        sp.dma_start(dst, pcs[2][0:DKV, :, :]).then_inc(pc_out[j], 16)
                if ch == 0:
                    sp.wait_ge(zero_rows, 2)
                    sp.wait_ge(pc_out[0], 16)
                    load_qop(0, 0)
                if ch == 2:
                    sp.wait_ge(pc_out[0], 16 * 3)
                    load_qop(0, 2)
                if hs == 1:
                    sp.wait_ge(pc_out[2], 16 * (ch + 1))
                    for k in range(PIECES):
                        src = kd[k, b].rearrange("(h d) t -> d h t", d=DH)
                        for a in range(PIECES):
                            r = DH * (PIECES * a + k)
                            sp.dma_start(kop[r:r + DH, b, :, :], src).then_inc(kop_in[b], 16)
                if ch == 1:
                    load_qop(0, 1)
            for j in range(2):
                sp.wait_ge(pc_out[j], 16 * CHUNKS)

            def move_max(i, c):
                sp.wait_ge(mt_copied, 4 * i + c + 1)
                for a in range(PIECES):
                    sp.dma_start(qop[MAX_ROW + a:MAX_ROW + a + 1, c, :, :].rearrange("o h s -> o (h s)"),
                                 mrow[PAIRS * a:PAIRS * (a + 1), c % 2, :]).then_inc(mrow_in[c], 16)

            def quad(i, c):
                if exists(i, c, 3):
                    if not is_first(i, c):
                        sp.wait_ge(score_b, TILES * (4 * i + c))
                    load_qop(*at(i, c, 3))
                if exists(i, c, 1):
                    move_max(*at(i, c, 1))

            move_max(0, 0)
            all_quads(sp, quad)

            for g in range(CHUNKS):
                b, _, tiles = chunk(g)
                for sts in out_parts(g):
                    sp.wait_ge(yout_done, TPC * g + sts.stop)
                    sp.dma_start(out_t[:, tiles, :][:, sts, :], yout[:, b, sts, :]).then_inc(out_done[b], 16)
            sp.wait_ge(out_done[0], 16 * 2)
            sp.wait_ge(out_done[1], 16 * 3)

        @block.gpsimd
        def _(pool):
            pool.memset(identf[:, :], 0.0).then_inc(ident_ready, 1)
            pool.wait_ge(ident_ready, 1)
            pool.affine_select(out=identf[:, :], in_=identf[:, :], compare_op=ALU.not_equal, fill=1.0,
                               base=0, pattern=[[-1, P]], channel_multiplier=1).then_inc(ident_ready, 1)
            pool.wait_ge(ident_ready, 2)
            pool.memset(memd[:, :], 0.0).then_inc(memd_zero, 1)
            pool.tensor_copy(identb[:, :], identf[:, :]).then_inc(const_ready, 1)
            pool.memset(vop[:, :, :, :, :], 0.0).then_inc(const_ready, 1)
            pool.wait_ge(const_ready, 2)
            pool.memset(vop[:, :, :, :, DH:DH + 1], 1.0).then_inc(const_ready, 1)
            pool.memset(ones[:, :], 1.0).then_inc(const_ready, 1)
            pool.memset(negexp[:, :], -0.5).then_inc(const_ready, 1)
            pool.memset(mpc[:, :, :], 0.0).then_inc(const_ready, 1)
            pool.memset(zeros[:, :], 0.0).then_inc(const_ready, 1)
            pool.memset(coarse[:, :], 1.0 / FINE).then_inc(const_ready, 1)
            pool.wait_ge(const_ready, CONSTS - 1)
            pool.memset(kop[MAX_ROW:ROWS, :, :, :], 1.0).then_inc(const_ready, 1)
            pool.wait_ge(const_ready, CONSTS)

            def add_mem(ch):
                for st in range(TPC):
                    n = TPC * ch + st
                    pool.wait_ge(mem_scaled, n + 1)
                    pool.tensor_tensor(xr[:, n, :], xr[:, n, :], amem[:, n % 2, :], ALU.add).then_inc(xr_done, 1)

            def split_max(i, c):
                q = 4 * i + c
                if not (isinstance(i, int) and q < 2):
                    pool.wait_ge(mt_ready, q - 1)
                pool.wait_ge(max_done, PAIRS * (q + 1))
                m, pc = mx[:, c % 2, :], mpc[:, c % 2, :]
                pool.tensor_tensor(pc[:, 0:PAIRS], m, zeros[:, :], ALU.add).then_inc(split_step, 1)
                pool.wait_ge(split_step, 4 * q + 1)
                pool.tensor_tensor(mrest[:, :], m, pc[:, 0:PAIRS], ALU.subtract).then_inc(split_step, 1)
                pool.wait_ge(split_step, 4 * q + 2)
                pool.tensor_tensor(pc[:, PAIRS:2 * PAIRS], mrest[:, :], zeros[:, :], ALU.add).then_inc(split_step, 1)
                pool.wait_ge(split_step, 4 * q + 3)
                pool.tensor_tensor(pc[:, 2 * PAIRS:3 * PAIRS], mrest[:, :], pc[:, PAIRS:2 * PAIRS], ALU.subtract).then_inc(split_step, 1)

            for ch in range(CHUNKS):
                for j in range(3):
                    np_ = P if j < 2 else DKV
                    pool.wait_ge(mid_done, 3 * ch + j + 1)
                    pool.tensor_tensor(pcs[j][0:np_, 2, :], rest[j][0:np_, :], pcs[j][0:np_, 1, :], ALU.subtract).then_inc(lo_done, 1)
                if ch == 1:
                    add_mem(0)
                    add_mem(1)
                if ch == 3:
                    split_max(0, 0)
                if ch > 1:
                    add_mem(ch)

            def ternary(w, part):
                if part == 0:
                    pool.wait_ge(f_in2, 16 * (w + 1))
                    pool.tensor_scalar(tneg[:, :], fraw[:, :], wscale[:, w, 2:3], None, ALU.is_lt).then_inc(tern_step, 1)
                    pool.tensor_scalar(tern[:, w, :], fraw[:, :], wscale[:, w, 1:2], None, ALU.is_gt).then_inc(tern_step, 1)
                else:
                    pool.wait_ge(tern_step, 3 * w + 2)
                    pool.tensor_tensor(tern[:, w, :], tern[:, w, :], tneg[:, :], ALU.subtract).then_inc(tern_step, 1)
                    pool.wait_ge(tern_step, 3 * w + 3)

            def quad(i, c):
                if exists(i, c, 1):
                    split_max(*at(i, c, 1))
                if isinstance(i, int) and i == 0:
                    if c == 0:
                        pool.wait_ge(fscale_step, 3)
                    ternary(c // 2, c % 2)
                if is_last(i) and c < 2:
                    ternary(2, c)

            all_quads(pool, quad)

            def rsqrt(n):
                pool.wait_ge(var_done, n + 1)
                pool.tensor_tensor(rstd[:, :], rstd[:, :], negexp[:, 0:TPC], ALU.pow).then_inc(rstd_done, 1)

            def low_pieces(g):
                for kc in range(KC):
                    pool.wait_ge(zrest_done, KC * g + kc + 1)
                    pool.tensor_tensor(zp[:, g % 2, 1, kc, :], zc[:, kc, :], coarse[:, :].broadcast_to([P, HALF]), ALU.mult).then_inc(zp_done, 1)

            def low_hidden(g, rs):
                for rr in rs:
                    n = ER * g + rr
                    pool.wait_ge(hrest_done, n + 1)
                    pool.tensor_tensor(hp[:, g % 2, 1, rr, :], hid[n % 3][:, :], coarse[:, :].broadcast_to([P, HALF]), ALU.mult).then_inc(hlo_done, 1)

            for g in range(3):
                rsqrt(g)
                if g == 1:
                    low_pieces(0)
            for g in range(CHUNKS):
                low_hidden(g, range(0, 3))
                if g + 1 < CHUNKS:
                    low_pieces(g + 1)
                low_hidden(g, [3, 4])
                rsqrt(3 + g)
                low_hidden(g, range(5, ER))
            rsqrt(7)
            rsqrt(8)

        @block.scalar
        def _(act):
            act.dma_start(fraw_to(0), f_dram[0]).then_inc(f_in, 16)
            for kc in range(KC):
                act.wait_ge(wt_ready, kc + 1)
                nc.scalar.activation(WT[:, kc, :], ps[:, kc, 0:3 * P], ACT.Copy).then_inc(wt_copied, 1)

            def copy_x(ch):
                for kc in range(KC):
                    act.wait_ge(xt_ready, KC * ch + kc + 1)
                    if ch >= 2:
                        act.wait_ge(proj_ready, 4 * (ch - 1))
                    nc.scalar.activation(xT[:, kc, ch % 2, :], ps[:, x_bank(ch, kc), :], ACT.Copy).then_inc(xt_copied, 1)

            def sum_weight(w):
                act.wait_ge(f_in, 16 * (w + 1))
                nc.scalar.activation(tern[:, w, :], fraw[:, :], ACT.Abs, accum_out=wsum[:, w:w + 1]).then_inc(fsum_done, 1)
                act.wait_ge(fsum_done, w + 1)
                if w < 2:
                    act.dma_start(fraw_to(w + 1), f_dram[w + 1]).then_inc(f_in, 16)

            copy_x(0)
            for ch in range(CHUNKS):
                b, hs = ch // 2, ch % 2
                for j in range(3):
                    np_ = P if j < 2 else DKV
                    act.wait_ge(proj_ready, 4 * ch + j + 1)
                    if ch:
                        act.wait_ge(pc_out[j], 16 * ch)
                    nc.scalar.activation(pcs[j][0:np_, 0, :], ps[0:np_, proj_bank(ch, j), :], ACT.Copy).then_inc(hi_done, 1)
                if ch == 0:
                    act.wait_ge(mw_in, 16)
                    nc.scalar.activation(w1[:, 1:2], w1[:, 0:1], ACT.Exp, scale=-1.0).then_inc(w_step, 1)
                    copy_x(1)
                for j in range(3):
                    np_ = P if j < 2 else DKV
                    act.wait_ge(rest_done, 3 * ch + j + 1)
                    nc.scalar.activation(pcs[j][0:np_, 1, :], rest[j][0:np_, :], ACT.Copy).then_inc(mid_done, 1)
                act.wait_ge(proj_ready, 4 * ch + 4)
                act.wait_ge(const_ready, CONSTS)
                nc.scalar.activation(vop[:, b, hs * TPC:(hs + 1) * TPC, :, 0:DH],
                                     ps[:, proj_bank(ch, 3), 0:TPC * DKV].rearrange("p (t h d) -> p t h d", t=TPC, h=NH),
                                     ACT.Copy).then_inc(v_done, 1)
                for j in range(2):
                    if ch:
                        act.wait_ge(sig_done, 2 * (ch - 1) + j + 1)
                    nc.scalar.activation(elu_e[j][:, :], ps[:, proj_bank(ch, j), :], ACT.Relu, scale=-1.0).then_inc(neg_done, 1)
                for j in range(2):
                    act.wait_ge(neg_done, 2 * ch + j + 1)
                    nc.scalar.activation(elu_e[j][:, :], elu_e[j][:, :], ACT.Exp, scale=-1.0).then_inc(exp_done, 1)
                if ch:
                    sum_weight(ch - 1)
                if ch in (1, 2):
                    copy_x(ch + 1)
            act.dma_start(fraw_to(0), f_dram[0]).then_inc(f_in2, 16)

            def high_pieces(g):
                for kc in range(KC):
                    act.wait_ge(zt_ready, KC * g + kc + 1)
                    if g >= 2:
                        act.wait_ge(gate_ready, ER * (g - 1))
                    nc.scalar.activation(zp[:, g % 2, 0, kc, :], ps[:, zbank(g, kc), :], ACT.Copy).then_inc(zhi_done, 1)

            def save_acc(i, c):
                q = 4 * i + c
                act.wait_ge(pv_done, TILES * (q + 1))
                if not (isinstance(i, int) and q < 2):
                    act.wait_ge(sel_ready, q - 1)
                nc.scalar.activation(acc_sb[:, c % 2, :], ps[:, ACC, :], ACT.Copy).then_inc(acc_saved, 1)

            def quad(i, c):
                q = 4 * i + c
                first = isinstance(i, int) and q == 0
                for t in range(TILES):
                    act.wait_ge(score_b, TILES * q + t + 1)
                    if not (first and t < PSLOTS):
                        act.wait_ge(pv_done, TILES * q + t + 1 - PSLOTS)
                    nc.scalar.activation(prob[:, t % PSLOTS, :], ps[:, 4 + slot_of(t) % 3, :], ACT.Exp,
                                         scale=SCALE).then_inc(prob_done, 1)
                    if t == HG - 1 and not first:
                        save_acc(*at(i, c, -1))
                    if t == 20 and is_last(i) and c == 3:
                        high_pieces(0)
                if isinstance(i, int) and i == 0 and c in (1, 3):
                    act.wait_ge(tern_step, 3 * (c // 2) + 2)
                    act.dma_start(fraw_to(c // 2 + 1), f_dram[c // 2 + 1]).then_inc(f_in2, 16)

            all_quads(act, quad)
            save_acc(ITERS - 1, 3)

            def high_hidden(n):
                g = n // ER
                act.wait_ge(hid_done, n + 1)
                if g >= 2:
                    act.wait_ge(down_ready, 2 * (g - 1))
                nc.scalar.activation(hp[:, g % 2, 0, n % ER, :], hid[n % 3][:, :], ACT.Copy).then_inc(hhi_done, 1)

            for g in range(CHUNKS):
                for r in range(ER):
                    n = ER * g + r
                    act.wait_ge(up_ready, n + 1)
                    if n >= 2:
                        act.wait_ge(hid_done, n - 1)
                    nc.scalar.activation(silu[r % 2][:, :], ps[:, r % 2, :], ACT.Silu,
                                         scale=wscale[:, 0, 0:1]).then_inc(silu_done, 1)
                    if n:
                        high_hidden(n - 1)
                    if r == 3 and g + 1 < CHUNKS:
                        high_pieces(g + 1)
            high_hidden(ER * CHUNKS - 1)

        @block.vector
        def _(dve):
            v = nc.vector
            v.memset(qop[64:MAX_ROW, :, :, :].rearrange("r c h s -> r (c h s)").bitcast(F32), 0.0).then_inc(zero_rows, 1)
            v.memset(kop[64:MAX_ROW, :, :, :].rearrange("r b h s -> r (b h s)").bitcast(F32), 0.0).then_inc(zero_rows, 1)
            def memory_weight_sigmoid():
                dve.wait_ge(w_step, 1)
                v.tensor_scalar(w1[:, 1:2], w1[:, 1:2], 1.0, None, ALU.add).then_inc(w_step, 1)
                dve.wait_ge(w_step, 2)
                v.reciprocal(w1[:, 2:3], w1[:, 1:2]).then_inc(w_step, 1)
                dve.wait_ge(w_step, 3)
                v.tensor_scalar(w1[:, 3:4], w1[:, 2:3], -1.0, 1.0, ALU.mult, ALU.add).then_inc(w_step, 1)
                dve.wait_ge(mem_in, 64)
                v.tensor_scalar(memd[:, 0:P], memd[:, 0:P], w1[:, 2:3], None, ALU.mult).then_inc(w_step, 1)

            def scale_mem(ch, st):
                n = TPC * ch + st
                num = ps[:, mem_bank(ch, st), 0:260].rearrange("p (f c) -> p f c", f=2)
                dve.wait_ge(mem_ready, n + 1)
                rm = rmem[:, n % 2, :].rearrange("p (f m) -> p f m", f=2)
                v.reciprocal(rm, num[:, :, P:P + 2]).then_inc(rm_step, 1)
                dve.wait_ge(rm_step, n + 1)
                if n >= 2:
                    dve.wait_ge(xr_done, n - 1)
                v.tensor_tensor(amem[:, n % 2, :].rearrange("p (f m k) -> p f m k", f=2, m=2),
                                num[:, :, 0:P].rearrange("p f (m k) -> p f m k", m=2),
                                rm.unsqueeze(3).broadcast_to([P, 2, 2, DKV]), ALU.mult).then_inc(mem_scaled, 1)

            def take_rest(ch, j):
                np_ = P if j < 2 else DKV
                dve.wait_ge(hi_done, 3 * ch + j + 1)
                if ch:
                    dve.wait_ge(lo_done, 3 * (ch - 1) + j + 1)
                v.tensor_tensor(rest[j][0:np_, :], ps[0:np_, proj_bank(ch, j), :], pcs[j][0:np_, 0, :], ALU.subtract).then_inc(rest_done, 1)

            def elu(ch):
                for j in range(2):
                    dve.wait_ge(exp_done, 2 * ch + j + 1)
                    v.tensor_scalar(elu_e[j][:, :], elu_e[j][:, :], -1.0, None, ALU.add).then_inc(em_done, 1)
                for j in range(2):
                    dve.wait_ge(em_done, 2 * ch + j + 1)
                    v.scalar_tensor_tensor(out=sig[j][:, :], in0=ps[:, proj_bank(ch, j), :], scalar=0.0, in1=elu_e[j][:, :],
                                           op0=ALU.max, op1=ALU.add).then_inc(sig_done, 1)

            def take_max(i, c, pairs):
                q = 4 * i + c
                for p in pairs:
                    dve.wait_ge(score_a, PAIRS * q + p + 1)
                    if p == 0 and not (isinstance(i, int) and q < 2):
                        dve.wait_ge(split_step, 4 * (q - 1))
                    v.tensor_reduce(mx[:, c % 2, p:p + 1], ps[:, 2 * (p % 2):2 * (p % 2) + 2, :],
                                    AX.XY, ALU.max, negate=True).then_inc(max_done, 1)

            def copy_mt(i, c):
                q = 4 * i + c
                dve.wait_ge(mt_ready, q + 1)
                if not (isinstance(i, int) and q < 2):
                    if isinstance(i, int) and i == 0:
                        dve.wait_ge(mrow_in[(c - 2) % 4], 16 * PIECES)
                    elif c >= 2:
                        dve.wait_ge(mrow_in[c - 2], 16 * PIECES * (i + 1))
                    else:
                        dve.wait_ge(mrow_in[c + 2], 16 * PIECES * i)
                v.tensor_copy(mrow[:, c % 2, :], ps[0:PIECES * PAIRS, MISC, 0:P // 2].bitcast(BF16)).then_inc(mt_copied, 1)

            def normalize(i, c):
                q = 4 * i + c
                sel = ps[:, MISC, SEL0:SEL0 + TPC * SELW].rearrange("p (t h w) -> p t h w", t=TPC, w=VW // 2)[:, :, 0:2 * HG - 1:2, :]
                dve.wait_ge(sel_ready, q + 1)
                v.reciprocal(rden[:, :, :], sel[:, :, :, DH]).then_inc(rden_done, 1)
                dve.wait_ge(rden_done, q + 1)
                v.tensor_tensor(attn[:, i, c // 2, :, HG * DH * (c % 2):HG * DH * (c % 2 + 1)].rearrange("p t (h d) -> p t h d", h=HG),
                                sel[:, :, :, 0:DH], rden[:, :, :].unsqueeze(3).broadcast_to([P, TPC, HG, DH]),
                                ALU.mult).then_inc(sel_used, 1)

            def quad(i, c):
                split = MISC_SLOT // 2 - HG * TPC // 2
                if exists(i, c, 1):
                    take_max(*at(i, c, 1), range(PAIRS // 2, PAIRS))
                if exists(i, c, 2):
                    take_max(*at(i, c, 2), range(0, split))
                if exists(i, c, 1):
                    copy_mt(*at(i, c, 1))
                if not is_first(i, c):
                    normalize(*at(i, c, -1))
                if exists(i, c, 2):
                    take_max(*at(i, c, 2), range(split, PAIRS // 2))
                if is_last(i) and c == 2:
                    copy_weights(0, 4)
                    norm_attention(0)
                    norm_attention(1)
                if is_last(i) and c == 3:
                    copy_weights(4, 2)
                    rest_pieces(0)
                    norm_attention(2)

            def copy_weights(k, n):
                for k in range(k, k + n):
                    dve.wait_ge(tt_ready, k + 1)
                    if k < 4:
                        dst, fine = upT[:, k // 2, k % 2, :], upT_fine[:, k // 2, k % 2, :]
                    else:
                        dst, fine = (t[:, 4 * (k - 4):4 * (k - 3), :].rearrange("p r d -> p (r d)") for t in (downT, downT_fine))
                    v.tensor_copy(dst, ps[:, k % 4, :].bitcast(BF16)).then_inc(tt_copied, 1)
                    dve.wait_ge(tt_copied, k + 1)
                    v.tensor_scalar(fine, dst, FINE, None, ALU.mult).then_inc(fine_done, 1)

            def norm_stats(n, y, sts):
                before = 8 * n if n < 8 else 8 * n - 4
                for st in sts:
                    v.bn_stats(stat[:, st, :], y[:, st, :]).then_inc(stat_done, 1)
                dve.wait_ge(stat_done, before + len(sts))
                for st in sts:
                    v.bn_aggr(mv[:, st, :], stat[:, st, :]).then_inc(stat_done, 1)
                dve.wait_ge(stat_done, before + 2 * len(sts))
                v.tensor_scalar(rstd[:, :], mv[:, :, 1], LN_EPS, None, ALU.add).then_inc(var_done, 1)

            def norm_apply(n, y, dst, done, sts):
                dve.wait_ge(rstd_done, n + 1)
                for st in sts:
                    v.tensor_scalar(dst[:, st, :], y[:, st, :], mv[:, st, 0:1], rstd[:, st:st + 1],
                                    ALU.subtract, ALU.mult).then_inc(done, 1)

            def add_attention(g):
                b, hs, tiles = chunk(g)
                y = xr[:, tiles, :]
                dve.wait_ge(sel_used, (30, 30, 31, QUADS)[g])
                for st in range(TPC):
                    yt = y[:, st, :].rearrange("p (n k) -> p n k", n=NQ)
                    v.scalar_tensor_tensor(out=yt, in0=attn[:, NQ * hs:NQ * (hs + 1), b, st, :], scalar=w1[:, 3:4], in1=yt,
                                           op0=ALU.mult, op1=ALU.add).then_inc(y_done, 1)

            def attention_stats(g):
                dve.wait_ge(y_done, TPC * (g + 1))
                norm_stats(g, xr[:, chunk(g)[2], :], range(TPC))

            def attention_apply(g):
                y = xr[:, chunk(g)[2], :]
                norm_apply(g, y, y, z_done, range(TPC))

            def norm_attention(g):
                add_attention(g)
                attention_stats(g)
                attention_apply(g)

            def rest_pieces(g):
                for kc in range(KC):
                    dve.wait_ge(zhi_done, KC * g + kc + 1)
                    if g:
                        dve.wait_ge(zp_done, KC * g)
                    v.tensor_tensor(zc[:, kc, :], ps[:, zbank(g, kc), :], zp[:, g % 2, 0, kc, :], ALU.subtract).then_inc(zrest_done, 1)

            def make_hidden(n):
                if n < ER * CHUNKS:
                    dve.wait_ge(gate_ready, n + 1)
                    dve.wait_ge(silu_done, n + 1)
                    if n >= 3:
                        dve.wait_ge(hlo_done, n - 2)
                    v.scalar_tensor_tensor(out=hid[n % 3][:, :], in0=ps[:, 2 + n % 2, :], scalar=hscale[:, 2:3],
                                           in1=silu[n % 2][:, :], op0=ALU.mult, op1=ALU.mult).then_inc(hid_done, 1)
                if n:
                    dve.wait_ge(hhi_done, n)
                    v.tensor_tensor(hid[(n - 1) % 3][:, :], hid[(n - 1) % 3][:, :], hp[:, (n - 1) // ER % 2, 0, (n - 1) % ER, :],
                                    ALU.subtract).then_inc(hrest_done, 1)

            def add_down(g, h):
                _, _, tiles = chunk(g)
                dve.wait_ge(down_ready, 2 * g + h + 1)
                zh = xr[:, tiles, :][:, 2 * h:2 * h + 2, :]
                product = ps[:, DOWN_BANKS[h], :].rearrange("p (t d) -> p t d", t=2) if g + 1 < CHUNKS else ps[:, 4 + 2 * h:6 + 2 * h, 0:DM]
                v.scalar_tensor_tensor(out=zh, in0=product,
                                       scalar=hscale[:, 3:4], in1=zh,
                                       op0=ALU.mult, op1=ALU.add).then_inc(y2_done, 1)

            def out_stats(g, sts):
                dve.wait_ge(y2_done, 2 * g + sts.stop // 2)
                norm_stats(CHUNKS + g + (sts.start > 0), xr[:, chunk(g)[2], :], range(sts.start, sts.stop))

            def out_apply(g, sts):
                b, _, tiles = chunk(g)
                if g >= 2:
                    dve.wait_ge(out_done[b], 16)
                norm_apply(CHUNKS + g + (sts.start > 0), xr[:, tiles, :], yout[:, b, :, :], yout_done, range(sts.start, sts.stop))

            for j in range(3):
                take_rest(0, j)
            memory_weight_sigmoid()
            elu(0)
            for j in range(3):
                take_rest(1, j)
            for st in range(TPC):
                scale_mem(0, st)
            elu(1)
            for st in range(TPC):
                scale_mem(1, st)
            take_max(0, 0, [0])
            for j in range(3):
                take_max(0, 0, [1 + j])
                take_rest(2, j)
            take_max(0, 0, [4])
            elu(2)
            take_max(0, 0, [5])
            for st in range(TPC):
                take_max(0, 0, [6 + st])
                scale_mem(2, st)
            take_max(0, 0, range(10, 13))
            for j in range(3):
                take_max(0, 0, [13 + j])
                take_rest(3, j)
            take_max(0, 1, range(0, 3))
            elu(3)
            take_max(0, 1, [3])
            for st in range(TPC):
                take_max(0, 1, [4 + st])
                scale_mem(3, st)
                if st == 0:
                    copy_mt(0, 0)
                if st == 2:
                    dve.wait_ge(fsum_all, 1)
                    v.tensor_scalar(wscale[:, :, 0], ps[:, MISC, 0:3], 1.0 / (DE * DM), Q_EPS, ALU.mult, ALU.add).then_inc(fscale_step, 1)
            dve.wait_ge(fscale_step, 1)
            v.tensor_scalar(wscale[:, :, 1], wscale[:, :, 0], 0.5, None, ALU.mult).then_inc(fscale_step, 1)
            v.tensor_scalar(wscale[:, :, 2], wscale[:, :, 0], -0.5, None, ALU.mult).then_inc(fscale_step, 1)
            v.reciprocal(hscale[:, 0:1], wscale[:, 0, 0:1]).then_inc(fscale_step, 1)
            v.tensor_tensor(hscale[:, 1:2], wscale[:, 0, 0:1], wscale[:, 1, 0:1], ALU.mult).then_inc(fscale_step, 1)
            dve.wait_ge(fscale_step, 5)
            v.tensor_scalar(hscale[:, 2:3], hscale[:, 0:1], HID, None, ALU.mult).then_inc(fscale_step, 1)
            v.tensor_scalar(hscale[:, 3:4], hscale[:, 1:2], wscale[:, 2, 0:1], 1.0 / HID, ALU.mult, ALU.mult).then_inc(fscale_step, 1)
            all_quads(dve, quad)

            full = slice(0, TPC)
            dve.wait_ge(fscale_step, 7)
            for g in range(CHUNKS):
                for r in range(4):
                    make_hidden(ER * g + r)
                if g:
                    for h in range(2):
                        add_down(g - 1, h)
                if g + 1 < CHUNKS:
                    rest_pieces(g + 1)
                make_hidden(ER * g + 4)
                if g == 0:
                    normalize(ITERS - 1, 3)
                    add_attention(3)
                make_hidden(ER * g + 5)
                if g:
                    out_stats(g - 1, full)
                else:
                    attention_stats(3)
                make_hidden(ER * g + 6)
                make_hidden(ER * g + 7)
                if g:
                    out_apply(g - 1, full)
                else:
                    attention_apply(3)
            make_hidden(ER * CHUNKS)
            for h, sts in enumerate(out_parts(CHUNKS - 1)):
                add_down(CHUNKS - 1, h)
                out_stats(CHUNKS - 1, sts)
                out_apply(CHUNKS - 1, sts)

        @block.tensor
        def _(pe):
            pe.wait_ge(ident_ready, 2)
            pe.wait_ge(w_in, 48)
            for kc in range(KC):
                for f in range(3):
                    last = pe.transpose(ps[:, kc, P * f:P * (f + 1)], wraw[:, f, P * kc:P * (kc + 1)], identf[:, :])
                last.then_inc(wt_ready, 1)

            def read_memory(ch, st):
                n = TPC * ch + st
                if st == 0:
                    pe.wait_ge(w_step, 5)
                    pe.wait_ge(sig_done, 2 * ch + 2)
                if n == 2 * TPC:
                    pe.wait_ge(rest_done, 3 * ch + 3)
                    pe.wait_ge(v_done, ch + 1)
                elif n == 3 * TPC:
                    pe.wait_ge(rest_done, 3 * ch + 3)
                    pe.wait_ge(v_done, ch + 1)
                elif n >= 2:
                    pe.wait_ge(mem_scaled, n - 1)
                for f in range(2):
                    last = pe.matmul(ps[:, mem_bank(ch, st), 130 * f:130 * (f + 1)], sig[f][:, P * st:P * (st + 1)],
                                     memd[:, :], start=True, stop=True)
                last.then_inc(mem_ready, 1)

            def turn_x(ch, kc):
                pe.wait_ge(x_in[ch], 16)
                if ch == 0:
                    pe.wait_ge(wt_copied, kc + 1)
                elif ch == 1:
                    pe.wait_ge(xt_copied, kc + 1)
                elif ch == 2:
                    pe.wait_ge(rest_done, 3 * ch)
                    pe.wait_ge(v_done, ch)
                else:
                    pe.wait_ge(mem_scaled, TPC * ch)
                for st in range(TPC):
                    last = pe.transpose(ps[:, x_bank(ch, kc), P * st:P * (st + 1)], xr[:, TPC * ch + st, P * kc:P * (kc + 1)], identf[:, :])
                last.then_inc(xt_ready, 1)

            def project(ch, j):
                np_ = P if j < 2 else DKV
                if j == 0:
                    pe.wait_ge(xt_copied, KC * (ch + 1))
                if j < 2 and ch >= 2:
                    pe.wait_ge(sig_done, 2 * (ch - 1) + j + 1)
                if j == 2 and ch == 1:
                    pe.wait_ge(rest_done, 3)
                for kc in range(KC):
                    last = pe.matmul(ps[0:np_, proj_bank(ch, j), :], WT[:, kc, P * j:P * j + np_], xT[:, kc, ch % 2, :],
                                     start=(kc == 0), stop=(kc == KC - 1))
                last.then_inc(proj_ready, 1)

            def project_v(ch):
                if ch == 1:
                    pe.wait_ge(v_done, 1)
                for st in range(TPC):
                    for kc in range(KC):
                        last = pe.matmul(ps[:, proj_bank(ch, 3), DKV * st:DKV * (st + 1)], xT[:, kc, ch % 2, P * st:P * (st + 1)],
                                         WT[:, kc, 2 * P + DKV:3 * P], start=(kc == 0), stop=(kc == KC - 1))
                last.then_inc(proj_ready, 1)

            def max_scores(i, c, pairs):
                q, b, hg = 4 * i + c, c // 2, c % 2
                for p in pairs:
                    j, st = p // TPC, p % TPC
                    if p == 0:
                        pe.wait_ge(qop_in[c], 16 * PIECES * PIECES * (i + 1))
                        if isinstance(i, int) and i == 0 and c % 2 == 0:
                            pe.wait_ge(kop_in[b], 16 * PIECES * PIECES)
                    if not (is_first(i, c) and p < 2):
                        pe.wait_ge(max_done, PAIRS * q + p - 1)
                    for half in range(2):
                        last = pe.matmul(ps[:, 2 * (p % 2) + half, :], qop[0:MAX_ROW, c, j, P * st:P * (st + 1)],
                                         kop[0:MAX_ROW, b, HG * hg + j, HALF * half:HALF * (half + 1)], start=True, stop=True)
                    last.then_inc(score_a, 1)

            def turn_max(i, c):
                q = 4 * i + c
                pe.wait_ge(split_step, 4 * (q + 1))
                pe.transpose(ps[:, MISC, 0:P // 2].bitcast(BF16), mpc[:, c % 2, :], identb[:, :]).then_inc(mt_ready, 1)

            def misc_read(i, c):
                if exists(i, c, 1):
                    pe.wait_ge(mt_copied, 4 * i + c + 2)
                if not is_first(i, c):
                    pe.wait_ge(sel_used, 4 * i + c)

            def scores(i, c, t):
                q, b, hg, tb, j = 4 * i + c, c // 2, c % 2, t // HG, t % HG
                if t == 0:
                    pe.wait_ge(mrow_in[c], 16 * PIECES * (i + 1))
                before = slot_of(t) - 3
                if before == MISC_SLOT:
                    misc_read(i, c)
                elif before >= 0 or not is_first(i, c):
                    pe.wait_ge(prob_done, TILES * q + before + 1 - (before > MISC_SLOT))
                pe.matmul(ps[:, 4 + slot_of(t) % 3, :], kop[0:ROWS, b, HG * hg + j, P * tb:P * (tb + 1)],
                          qop[0:ROWS, c, j, :], start=True, stop=True).then_inc(score_b, 1)

            def times_v(i, c, tb):
                q, b, hg = 4 * i + c, c // 2, c % 2
                if tb == 0:
                    pe.wait_ge(acc_saved, q)
                for j in range(HG):
                    t = HG * tb + j
                    pe.wait_ge(prob_done, TILES * q + t + 1)
                    pe.matmul(ps[VW * j:VW * (j + 1), ACC, :], vop[:, b, tb, HG * hg + j, :], prob[:, t % PSLOTS, :],
                              start=(tb == 0), stop=(tb == TB - 1)).then_inc(pv_done, 1)

            def down_last(g):
                pe.wait_ge(y2_done, 2 * g)
                pe.wait_ge(zrest_done, KC * CHUNKS)
                for r in range(ER):
                    pe.wait_ge(hlo_done, ER * g + r + 1)
                    for st in range(TPC):
                        for e, wt in ((0, downT), (1, downT_fine)):
                            last = pe.matmul(ps[:, 4 + st, 0:DM], hp[:, g % 2, e, r, P * st:P * (st + 1)], wt[:, r, :],
                                             start=(r == 0 and e == 0), stop=(r == ER - 1 and e == 1))
                        if r == ER - 1 and st % 2:
                            last.then_inc(down_ready, 1)

            def select(i, c):
                q = 4 * i + c
                pe.wait_ge(acc_saved, q + 1)
                for st in range(TPC):
                    last = pe.transpose(ps[:, MISC, SEL0 + SELW * st:SEL0 + SELW * (st + 1)],
                                        acc_sb[0:SELW, c % 2, P * st:P * (st + 1)], identf[0:SELW, 0:SELW])
                last.then_inc(sel_ready, 1)

            def quad(i, c):
                for tb in range(TB):
                    ahead, first = (1, PAIRS // 2 + 2 * tb) if tb < TB // 2 else (2, 2 * tb - TB)
                    scores(i, c, HG * tb)
                    if exists(i, c, ahead):
                        max_scores(*at(i, c, ahead), [first])
                    scores(i, c, HG * tb + 1)
                    scores(i, c, HG * tb + 2)
                    if exists(i, c, ahead):
                        max_scores(*at(i, c, ahead), [first + 1])
                    scores(i, c, HG * tb + 3)
                    if is_last(i) and c == 2 and tb in (4, 6):
                        turn_up_gate(tb // 2 - 2)
                    if is_last(i) and c == 3 and tb == 1:
                        turn_down()
                    if is_last(i) and c == 3 and tb == 2:
                        turn_rows(0)
                    if HG * (tb + 1) == MISC_SLOT:
                        pe.wait_ge(prob_done, TILES * (4 * i + c) + MISC_SLOT - 2)
                        if not is_first(i, c):
                            select(*at(i, c, -1))
                        if exists(i, c, 1):
                            turn_max(*at(i, c, 1))
                    if tb:
                        times_v(i, c, tb - 1)
                    elif not is_first(i, c):
                        times_v(*at(i, c, -1), TB - 1)

            def turn_up_gate(w):
                pe.wait_ge(tern_step, 9)
                pe.wait_ge(max_done, PAIRS * QUADS)
                for kc in range(KC):
                    for r in range(ER):
                        last = pe.transpose(ps[:, KC * w + kc, :].bitcast(BF16)[:, P * r:P * (r + 1)],
                                            tern[:, w, DM * r + P * kc:DM * r + P * (kc + 1)], identb[:, :])
                    last.then_inc(tt_ready, 1)

            def turn_down():
                pe.wait_ge(tt_copied, 2)
                tdown = tern[:, 2, :].rearrange("p (k e r) -> p k e r", k=KC, r=ER)
                for h in range(2):
                    for r in range(4):
                        for kc in range(KC):
                            last = pe.transpose(ps[:, h, :].bitcast(BF16)[:, DM * r + P * kc:DM * r + P * (kc + 1)],
                                                tdown[:, kc, :, 4 * h + r], identb[:, :])
                    last.then_inc(tt_ready, 1)

            def turn_rows(g):
                _, _, tiles = chunk(g)
                pe.wait_ge(z_done, TPC * (g + 1))
                if g == 0:
                    pe.wait_ge(tt_copied, 4)
                elif g > 1:
                    pe.wait_ge(zrest_done, KC * g)
                for kc in range(KC):
                    for st in range(TPC):
                        last = pe.transpose(ps[:, zbank(g, kc), P * st:P * (st + 1)],
                                            xr[:, tiles, :][:, st, P * kc:P * (kc + 1)], identf[:, :])
                    last.then_inc(zt_ready, 1)

            def up_gate(g, rs):
                for r in rs:
                    n = ER * g + r
                    if r == 0:
                        pe.wait_ge(zp_done, KC * (g + 1))
                    if n == 0:
                        pe.wait_ge(fine_done, 6)
                    if n >= 2:
                        pe.wait_ge(hid_done, n - 1)
                    for w, ready in ((0, up_ready), (1, gate_ready)):
                        for kc in range(KC):
                            for e, wt in ((0, upT), (1, upT_fine)):
                                last = pe.matmul(ps[:, 2 * w + r % 2, :], wt[:, w, kc, P * r:P * (r + 1)], zp[:, g % 2, e, kc, :],
                                                 start=(kc == 0 and e == 0), stop=(kc == KC - 1 and e == 1))
                        last.then_inc(ready, 1)

            def down(g):
                pe.wait_ge(hlo_done, ER * (g + 1))
                if g:
                    pe.wait_ge(y2_done, 2 * g)
                else:
                    pe.wait_ge(sel_used, QUADS)
                    pe.wait_ge(acc_saved, QUADS)
                for st in range(TPC):
                    for r in range(ER):
                        for e, wt in ((0, downT), (1, downT_fine)):
                            last = pe.matmul(ps[:, DOWN_BANKS[st // 2], DM * (st % 2):DM * (st % 2 + 1)],
                                             hp[:, g % 2, e, r, P * st:P * (st + 1)], wt[:, r, :],
                                             start=(r == 0 and e == 0), stop=(r == ER - 1 and e == 1))
                    if st % 2:
                        last.then_inc(down_ready, 1)

            for ch in range(2):
                for kc in range(KC):
                    turn_x(ch, kc)
                for j in range(3):
                    project(ch, j)
                project_v(ch)
            for st in range(TPC):
                read_memory(0, st)
            for kc in range(KC):
                turn_x(2, kc)
            for st in range(TPC):
                read_memory(1, st)
            pe.wait_ge(mem_scaled, 2 * TPC)
            max_scores(0, 0, [0, 1])
            for j in range(3):
                project(2, j)
                max_scores(0, 0, [2 + j])
            project_v(2)
            max_scores(0, 0, [5])
            for st in range(TPC):
                max_scores(0, 0, [6 + st])
                read_memory(2, st)
            for kc in range(KC):
                max_scores(0, 0, [10 + kc])
                turn_x(3, kc)
            for j in range(3):
                max_scores(0, 0, [12 + j])
                project(3, j)
            max_scores(0, 0, [15])
            project_v(3)
            max_scores(0, 1, range(0, 4))
            for st in range(TPC):
                max_scores(0, 1, [4 + st])
                read_memory(3, st)
                if st == 0:
                    pe.wait_ge(const_ready, CONSTS)
                    turn_max(0, 0)
                if st == 2:
                    pe.wait_ge(mt_copied, 1)
                    pe.wait_ge(fsum_done, 3)
                    pe.matmul(ps[:, MISC, 0:3], ones[:, :], wsum[:, :], start=True, stop=True).then_inc(fsum_all, 1)
            pe.wait_ge(fscale_step, 1)
            pe.wait_ge(mem_scaled, TPC * CHUNKS)
            all_quads(pe, quad)
            times_v(ITERS - 1, 3, TB - 1)
            pe.wait_ge(prob_done, TILES * QUADS)

            for g in range(CHUNKS):
                up_gate(g, range(0, 4))
                if g:
                    down(g - 1)
                else:
                    select(ITERS - 1, 3)
                if g + 1 < CHUNKS:
                    turn_rows(g + 1)
                up_gate(g, range(4, ER))
            down_last(CHUNKS - 1)


_INS = ["L0_attn_x", "L0_attn_Wq", "L0_attn_Wk", "L0_attn_Wv", "L0_attn_memory", "L0_attn_memory_norm",
        "L0_attn_memory_weight", "L0_ffn_W_up", "L0_ffn_W_gate", "L0_ffn_W_down"]


def kernel(**inputs):
    import numpy as _np
    import concourse.bacc as _bacc
    from concourse import mybir as _mybir
    from concourse.bass_utils import run_bass_kernel_spmd as _run

    nc = _bacc.Bacc("TRN2", target_bir_lowering=False, num_devices=1)
    arrays, args = {}, []
    for name in _INS:
        a = _np.ascontiguousarray(inputs[name])
        arrays[f"in_{name}"] = a
        args.append(nc.dram_tensor(f"in_{name}", a.shape, _mybir.dt.from_np(a.dtype), kind="ExternalInput").ap())
    args.append(nc.dram_tensor("out_0", (2, 1024, 256), _mybir.dt.float32, kind="ExternalOutput").ap())
    attention_ffn_kernel(nc, *args)
    r = _run(nc, [arrays], core_ids=[0])
    return r.results[0]["out_0"]
```

```python
from contextlib import ExitStack

import concourse.bass as bass
from concourse import mybir

F32 = mybir.dt.float32
BF16 = mybir.dt.bfloat16
FP16 = mybir.dt.float16
ALU = mybir.AluOpType
ACT = mybir.ActivationFunctionType
AX = mybir.AxisListType

P = 128
BATCH, SEQ, DM = 2, 1024, 256
NQ, NH, DH = 4, 8, 8
DKV = NH * DH
DE = 1024
SCALE = float(1.0 / (DH ** 0.5))
LN_EPS = 1e-5
Q_EPS = 1e-8
PIECES = 3
HALF = 512
CHUNKS = BATCH * SEQ // HALF
TPC = HALF // P
KC = DM // P
PROD_ROWS = PIECES * PIECES * DH
MAX_ROW = 96
ROWS = MAX_ROW + PIECES
TB = SEQ // P
HG = 4
ITERS = (SEQ // HALF) * NQ
QUADS = 4 * ITERS
TILES = TB * HG
PAIRS = HG * TPC
VW = 32
SELW = (HG - 1) * VW + VW // 2
PSLOTS = 16
JOBS = (2, 0, 1)
ER = DE // P
CONSTS = 6
ONE_PAIR = 1.0 + 0x3F80 / 2 ** 23
FINE = 2.0 ** -11
HID = 2.0 ** -8


def attention_ffn_kernel(nc, x, Wq, Wk, Wv, memory, memory_norm, memory_weight, W_up, W_gate, W_down, out):
    with ExitStack() as ctx:
        def sb(name, shape, dt=F32):
            return ctx.enter_context(nc.sbuf_tensor(name, shape, dt))

        def sem(name):
            return ctx.enter_context(nc.semaphore(name))

        xr = sb("xr", [P, BATCH * SEQ // P, DM])
        attn = sb("attn", [P, ITERS, BATCH, TPC, 2 * HG * DH])
        vop = sb("vop", [P, BATCH, TB, NH, VW])
        kop = sb("kop", [P, BATCH, NH, SEQ], BF16)
        qop = sb("qop", [P, 4, HG, HALF], BF16)
        prob = sb("prob", [P, PSLOTS, HALF])
        acc_sb = sb("acc_sb", [P, 2, HALF])
        identf = sb("identf", [P, P])
        identb = sb("identb", [P, P], BF16)
        ones = sb("ones", [P, P])
        mx = sb("mx", [P, 2, PAIRS])
        mrest = sb("mrest", [P, PAIRS])
        mpc = sb("mpc", [P, 2, P], BF16)
        mrow = sb("mrow", [PIECES * PAIRS, 2, P], BF16)
        rden = sb("rden", [P, TPC, HG])
        w1 = sb("w1", [P, 4])
        wraw = sb("wraw", [P, 3, DM])
        WT = sb("WT", [P, KC, 3 * P])
        memd = sb("memd", [P, 130])
        pcs = [sb(f"pcs{j}", [P, PIECES, HALF], BF16) for j in range(3)]
        rest = [sb(f"rest{j}", [P, HALF]) for j in range(3)]
        elu_e = [sb(f"elu_e{j}", [P, HALF]) for j in range(2)]
        sig = [sb(f"sig{j}", [P, HALF]) for j in range(2)]
        amem = sb("amem", [P, 2, DM])
        rmem = sb("rmem", [P, 2, 4])
        xT = prob[:, 0:4, :].rearrange("p (k c) s -> p k c s", k=KC)
        fraw = sb("fraw", [P, ER * DM])
        tern = sb("tern", [P, 3, ER * DM], BF16)
        tneg = sb("tneg", [P, ER * DM], BF16)
        wsum = sb("wsum", [P, 3])
        wscale = sb("wscale", [P, 3, 3])
        upT = sb("upT", [P, 2, KC, DE], BF16)
        upT_fine = sb("upT_fine", [P, 2, KC, DE], BF16)
        downT = kop[:, 0, 0:2, :].rearrange("p h s -> p (h s)").rearrange("p (r d) -> p r d", r=ER)
        downT_fine = kop[:, 0, 2:4, :].rearrange("p h s -> p (h s)").rearrange("p (r d) -> p r d", r=ER)
        zp = kop[:, 0, 4:8, :].rearrange("p h s -> p (h s)").bitcast(FP16).rearrange("p (b e k s) -> p b e k s", b=2, e=2, k=KC)
        yout = kop[:, 1, 0:4, :].rearrange("p h s -> p (h s)").bitcast(F32).rearrange("p (b t d) -> p b t d", b=2, t=TPC)
        hid = rest
        hp = prob[:, :, :].rearrange("p t s -> p (t s)").bitcast(FP16).rearrange("p (b e r s) -> p b e r s", b=2, e=2, r=ER)
        hscale = sb("hscale", [P, 4])
        silu = elu_e
        stat = sb("stat", [P, TPC, 6])
        mv = sb("mv", [P, TPC, 2])
        rstd = sb("rstd", [P, TPC])
        negexp = sb("negexp", [P, TPC])
        zeros = sb("zeros", [P, PAIRS])
        coarse = sb("coarse", [P, 1])
        zc = fraw[:, 0:KC * HALF].rearrange("p (k s) -> p k s", k=KC)

        ps = ctx.enter_context(nc.psum_tensor("ps", [P, 8, HALF], F32))
        DOWN_BANKS = (6, 7)
        ACC, MISC_SLOT, SEL0 = 7, 20, 64
        MISC = 4 + MISC_SLOT % 3

        def nth(j):
            return JOBS.index(j) + 1

        def x_bank(ch, kc):
            return kc if ch < 2 else 4 + kc

        def proj_bank(ch, j):
            return ((2, 3, 4, 5), (6, 7, 4, 5), (6, 7, 5, 4), (6, 7, 5, 4))[ch][j]

        def mem_bank(ch, st):
            return st % 2 if ch == 0 else 4 + st % 2

        def slot_of(t):
            return t + (t >= MISC_SLOT)

        qd = nc.dram_tensor("q_pieces", (PIECES, BATCH, ITERS, DKV, HALF), BF16, kind="Internal").ap()
        kd = nc.dram_tensor("k_pieces", (PIECES, BATCH, DKV, SEQ), BF16, kind="Internal").ap()

        x_in = [sem(f"x_in{c}") for c in range(CHUNKS)]
        zero_rows = sem("zero_rows")
        memd_zero, w_in, mem_in, mw_in = sem("memd_zero"), sem("w_in"), sem("mem_in"), sem("mw_in")
        ident_ready, const_ready = sem("ident_ready"), sem("const_ready")
        ops_set = sem("ops_set")
        wt_ready, wt_copied = sem("wt_ready"), sem("wt_copied")
        xt_ready, xt_copied = sem("xt_ready"), sem("xt_copied")
        proj_ready, hi_done, v_done = sem("proj_ready"), sem("hi_done"), sem("v_done")
        rest_done, mid_done, lo_done = sem("rest_done"), sem("mid_done"), sem("lo_done")
        neg_done, exp_done, em_done, sig_done = sem("neg_done"), sem("exp_done"), sem("em_done"), sem("sig_done")
        pc_out = [sem(f"pc_out{j}") for j in range(3)]
        mem_ready, mem_scaled, xr_done = sem("mem_ready"), sem("mem_scaled"), sem("xr_done")
        w_step, rm_step = sem("w_step"), sem("rm_step")
        kop_in = [sem(f"kop_in{c}") for c in range(4)]
        qop_in = [sem(f"qop_in{c}") for c in range(4)]
        mrow_in = [sem(f"mrow_in{c}") for c in range(4)]
        score_a, max_done = sem("score_a"), sem("max_done")
        split_step, mt_ready, mt_copied = sem("split_step"), sem("mt_ready"), sem("mt_copied")
        score_b, prob_done, pv_done = sem("score_b"), sem("prob_done"), sem("pv_done")
        acc_saved, sel_ready, rden_done, sel_used = sem("acc_saved"), sem("sel_ready"), sem("rden_done"), sem("sel_used")
        f_in, fsum_done, fsum_all, fscale_step = sem("f_in"), sem("fsum_done"), sem("fsum_all"), sem("fscale_step")
        f_in2, tern_step = sem("f_in2"), sem("tern_step")
        tt_ready, tt_copied, fine_done = sem("tt_ready"), sem("tt_copied"), sem("fine_done")
        y_done, stat_done, var_done, rstd_done = sem("y_done"), sem("stat_done"), sem("var_done"), sem("rstd_done")
        z_done, zt_ready, zhi_done, zrest_done, zp_done = sem("z_done"), sem("zt_ready"), sem("zhi_done"), sem("zrest_done"), sem("zp_done")
        up_ready, gate_ready, silu_done, hid_done = sem("up_ready"), sem("gate_ready"), sem("silu_done"), sem("hid_done")
        hhi_done, hrest_done, hlo_done = sem("hhi_done"), sem("hrest_done"), sem("hlo_done")
        down_ready, y2_done, yout_done = sem("down_ready"), sem("y2_done"), sem("yout_done")
        out_done = [sem(f"out_done{b}") for b in range(BATCH)]

        x_t = x.rearrange("b (t p) d -> p (b t) d", p=P)
        out_t = out.rearrange("b (t p) d -> p (b t) d", p=P)
        f_dram = [W_up.rearrange("(p r) d -> p (r d)", r=ER), W_gate.rearrange("(p r) d -> p (r d)", r=ER),
                  W_down.rearrange("(c p) e -> p c e", p=P)]

        def fraw_to(w):
            return fraw[:, :].rearrange("p (c e) -> p c e", c=KC) if w == 2 else fraw[:, :]

        def at(i, c, k):
            return i + (c + k) // 4, (c + k) % 4

        def is_last(i):
            return isinstance(i, int) and i == ITERS - 1

        def chunk(g):
            b, hs = g % 2, g // 2
            return b, hs, slice(TB * b + TPC * hs, TB * b + TPC * (hs + 1))

        def out_parts(g):
            return [slice(0, TPC)] if g + 1 < CHUNKS else [slice(0, 2), slice(2, TPC)]

        def zbank(g, kc):
            return (2 if g == 0 else 4) + kc

        def is_first(i, c):
            return isinstance(i, int) and 4 * i + c == 0

        def exists(i, c, k):
            return not isinstance(i, int) or 4 * i + c + k < QUADS

        def all_quads(eng, quad):
            for c in range(4):
                quad(0, c)
            with eng.Fori(1, ITERS - 1) as i:
                for c in range(4):
                    quad(i, c)
            for c in range(4):
                quad(ITERS - 1, c)

        block = ctx.enter_context(nc.Block())

        @block.sync
        def _(sp):
            sp.dma_start(wraw[:, 0:2, :], Wq.rearrange("(c p) d -> p c d", p=P)).then_inc(w_in, 16)
            sp.dma_start(wraw[0:DKV, 2, :], Wk).then_inc(w_in, 16)
            sp.dma_start(wraw[DKV:P, 2, :], Wv).then_inc(w_in, 16)
            for ch in range(CHUNKS):
                sp.dma_start(xr[:, TPC * ch:TPC * (ch + 1), :], x_t[:, TPC * ch:TPC * (ch + 1), :]).then_inc(x_in[ch], 16)

            sp.wait_ge(memd_zero, 1)
            for k in range(2):
                for src, cols in ((memory, slice(DKV * k, DKV * (k + 1))), (memory_norm, slice(P + k, P + k + 1))):
                    sp.dma_start(memd[DKV * k:DKV * (k + 1), cols], src.rearrange("(h d) m -> d h m", d=DH),
                                 allow_slow_non_contiguous=True).then_inc(mem_in, 16)
            sp.dma_start(w1[:, 0:1], memory_weight.rearrange("(o n) -> o n", o=1).broadcast_to([P, 1])).then_inc(mw_in, 16)

            def load_qop(i, c):
                b, hg = c // 2, c % 2
                for a in range(PIECES):
                    src = qd[a, b, i].rearrange("(d h) s -> d (h s)", d=DH)[:, HG * HALF * hg:HG * HALF * (hg + 1)]
                    rows = slice(DH * PIECES * a, DH * PIECES * (a + 1))
                    sp.dma_start(qop[rows, c, :, :].rearrange("r h s -> r (h s)"),
                                 src.unsqueeze(0).broadcast_to([PIECES, DH, HG * HALF])).then_inc(qop_in[c], 16)

            def move_max(i, c):
                sp.wait_ge(mt_copied, 4 * i + c + 1)
                sp.dma_start(qop[MAX_ROW:ROWS, c, :, :].rearrange("a h s -> a (h s)"), mrow[:, c % 2, :]).then_inc(mrow_in[c], 16)

            def load_kop(b):
                sp.wait_ge(pc_out[2], 32 * (b + 1))
                for hg in range(NH // HG):
                    src = kd[:, b].rearrange("k (d h) t -> k d (h t)", d=DH)[:, :, HG * SEQ * hg:HG * SEQ * (hg + 1)]
                    for a in range(PIECES):
                        rows = slice(DH * PIECES * a, DH * PIECES * (a + 1))
                        sp.dma_start(kop[rows, b, HG * hg:HG * (hg + 1), :].rearrange("r h t -> r (h t)"), src).then_inc(kop_in[2 * b + hg], 16)

            for ch in range(CHUNKS):
                b, hs = ch // 2, ch % 2
                if ch == 0:
                    sp.wait_ge(zero_rows, 2)
                if ch == 3:
                    move_max(0, 0)
                for j in JOBS:
                    sp.wait_ge(lo_done, 3 * ch + nth(j))
                    if j == 1 and hs == 1:
                        load_kop(b)
                    if j < 2:
                        dst = qd[:, b, hs * NQ + 2 * j:hs * NQ + 2 * j + 2].rearrange("a n f s -> (n f) a s")
                        sp.dma_start(dst, pcs[j][:, :, :]).then_inc(pc_out[j], 16)
                    else:
                        dst = kd[:, b, :, hs * HALF:(hs + 1) * HALF].rearrange("a f s -> f a s")
                        sp.dma_start(dst, pcs[2][0:DKV, :, :]).then_inc(pc_out[j], 16)
                if ch == 0:
                    sp.wait_ge(pc_out[0], 16)
                    load_qop(0, 0)
                if ch == 1:
                    load_qop(0, 1)
                if ch == 2:
                    sp.wait_ge(pc_out[0], 16 * 3)
                    load_qop(0, 2)
            for j in range(2):
                sp.wait_ge(pc_out[j], 16 * CHUNKS)

            def quad(i, c):
                if exists(i, c, 3):
                    if not is_first(i, c):
                        sp.wait_ge(score_b, TILES * (4 * i + c))
                    load_qop(*at(i, c, 3))
                if exists(i, c, 1):
                    move_max(*at(i, c, 1))

            all_quads(sp, quad)

            for g in range(CHUNKS):
                b, _, tiles = chunk(g)
                for sts in out_parts(g):
                    sp.wait_ge(yout_done, TPC * g + sts.stop)
                    sp.dma_start(out_t[:, tiles, :][:, sts, :], yout[:, b, sts, :]).then_inc(out_done[b], 16)
            sp.wait_ge(out_done[0], 16 * 2)
            sp.wait_ge(out_done[1], 16 * 3)

        @block.gpsimd
        def _(pool):
            pool.memset(identf[:, :], 0.0).then_inc(ident_ready, 1)
            pool.wait_ge(ident_ready, 1)
            pool.affine_select(out=identf[:, :], in_=identf[:, :], compare_op=ALU.not_equal, fill=1.0,
                               base=0, pattern=[[-1, P]], channel_multiplier=1).then_inc(ident_ready, 1)
            pool.wait_ge(ident_ready, 2)
            pool.memset(memd[:, :], 0.0).then_inc(memd_zero, 1)
            pool.tensor_copy(identb[:, :], identf[:, :]).then_inc(const_ready, 1)
            pool.memset(ones[:, :], 1.0).then_inc(const_ready, 1)
            pool.memset(negexp[:, :], -0.5).then_inc(const_ready, 1)
            pool.memset(mpc[:, :, :], 0.0).then_inc(const_ready, 1)
            pool.memset(zeros[:, :], 0.0).then_inc(const_ready, 1)
            pool.memset(coarse[:, :], 1.0 / FINE).then_inc(const_ready, 1)

            def set_operands(b):
                pool.memset(vop[:, b, :, :, DH:DH + 1], 1.0).then_inc(ops_set, 1)
                pool.memset(vop[:, b, :, :, DH + 1:VW], 0.0).then_inc(ops_set, 1)
                pool.wait_ge(ops_set, 3 * b + 2)
                pool.memset(kop[MAX_ROW:ROWS, b, :, :].rearrange("r h s -> r (h s)").bitcast(F32), ONE_PAIR).then_inc(ops_set, 1)
                pool.wait_ge(ops_set, 3 * b + 3)

            pool.wait_ge(const_ready, CONSTS)
            set_operands(0)

            def add_mem(ch):
                for st in range(TPC):
                    n = TPC * ch + st
                    pool.wait_ge(mem_scaled, n + 1)
                    pool.tensor_tensor(xr[:, n, :], xr[:, n, :], amem[:, n % 2, :], ALU.add).then_inc(xr_done, 1)

            def split_max(i, c):
                q = 4 * i + c
                if not (isinstance(i, int) and q < 2):
                    pool.wait_ge(mt_ready, q - 1)
                pool.wait_ge(max_done, PAIRS * (q + 1))
                m, pc = mx[:, c % 2, :], mpc[:, c % 2, :]
                pool.tensor_tensor(pc[:, 0:PAIRS], m, zeros[:, :], ALU.add).then_inc(split_step, 1)
                pool.wait_ge(split_step, 4 * q + 1)
                pool.tensor_tensor(mrest[:, :], m, pc[:, 0:PAIRS], ALU.subtract).then_inc(split_step, 1)
                pool.wait_ge(split_step, 4 * q + 2)
                pool.tensor_tensor(pc[:, PAIRS:2 * PAIRS], mrest[:, :], zeros[:, :], ALU.add).then_inc(split_step, 1)
                pool.wait_ge(split_step, 4 * q + 3)
                pool.tensor_tensor(pc[:, 2 * PAIRS:3 * PAIRS], mrest[:, :], pc[:, PAIRS:2 * PAIRS], ALU.subtract).then_inc(split_step, 1)

            for ch in range(CHUNKS):
                if ch == 3:
                    split_max(0, 0)
                for j in JOBS:
                    np_ = P if j < 2 else DKV
                    pool.wait_ge(mid_done, 3 * ch + nth(j))
                    pool.tensor_tensor(pcs[j][0:np_, 2, :], rest[j][0:np_, :], pcs[j][0:np_, 1, :], ALU.subtract).then_inc(lo_done, 1)
                if ch == 1:
                    add_mem(0)
                    add_mem(1)
                if ch > 1:
                    add_mem(ch)

            def ternary(w, part):
                if part == 0:
                    pool.wait_ge(f_in2, 16 * (w + 1))
                    pool.tensor_scalar(tneg[:, :], fraw[:, :], wscale[:, w, 2:3], None, ALU.is_lt).then_inc(tern_step, 1)
                    pool.tensor_scalar(tern[:, w, :], fraw[:, :], wscale[:, w, 1:2], None, ALU.is_gt).then_inc(tern_step, 1)
                else:
                    pool.wait_ge(tern_step, 3 * w + 2)
                    pool.tensor_tensor(tern[:, w, :], tern[:, w, :], tneg[:, :], ALU.subtract).then_inc(tern_step, 1)
                    pool.wait_ge(tern_step, 3 * w + 3)

            def quad(i, c):
                if exists(i, c, 1):
                    split_max(*at(i, c, 1))
                if isinstance(i, int) and i == 0:
                    if c == 0:
                        pool.wait_ge(fscale_step, 3)
                    ternary(c // 2, c % 2)
                if is_last(i) and c < 2:
                    ternary(2, c)

            set_operands(1)
            all_quads(pool, quad)

            def rsqrt(n, sts=slice(0, TPC)):
                pool.wait_ge(var_done, n + 1)
                pool.tensor_tensor(rstd[:, sts], rstd[:, sts], negexp[:, sts], ALU.pow).then_inc(rstd_done, 1)

            def low_pieces(g):
                for kc in range(KC):
                    pool.wait_ge(zrest_done, KC * g + kc + 1)
                    pool.tensor_tensor(zp[:, g % 2, 1, kc, :], zc[:, kc, :], coarse[:, :].broadcast_to([P, HALF]), ALU.mult).then_inc(zp_done, 1)

            def low_hidden(g, rs):
                for rr in rs:
                    n = ER * g + rr
                    pool.wait_ge(hrest_done, n + 1)
                    pool.tensor_tensor(hp[:, g % 2, 1, rr, :], hid[n % 3][:, :], coarse[:, :].broadcast_to([P, HALF]), ALU.mult).then_inc(hlo_done, 1)

            for g in range(3):
                rsqrt(g)
                if g == 1:
                    low_pieces(0)
            for g in range(CHUNKS):
                low_hidden(g, range(0, 3))
                if g + 1 < CHUNKS:
                    low_pieces(g + 1)
                low_hidden(g, [3, 4])
                rsqrt(3 + g)
                low_hidden(g, range(5, ER))
            for h, sts in enumerate(out_parts(CHUNKS - 1)):
                rsqrt(2 * CHUNKS - 1 + h, sts)

        @block.scalar
        def _(act):
            act.dma_start(fraw_to(0), f_dram[0]).then_inc(f_in, 16)
            for kc in range(KC):
                act.wait_ge(wt_ready, kc + 1)
                nc.scalar.activation(WT[:, kc, 0:DM + DKV].rearrange("p (n d h) -> p n h d", d=DH, h=NH),
                                     ps[:, kc, 0:DM + DKV].rearrange("p (n h d) -> p n h d", d=DH, h=NH), ACT.Copy).then_inc(wt_copied, 1)
                nc.scalar.activation(WT[:, kc, DM + DKV:3 * P], ps[:, kc, DM + DKV:3 * P], ACT.Copy).then_inc(wt_copied, 1)

            def copy_x(ch):
                for kc in range(KC):
                    act.wait_ge(xt_ready, KC * ch + kc + 1)
                    if ch >= 2:
                        act.wait_ge(proj_ready, 4 * (ch - 1))
                    nc.scalar.activation(xT[:, kc, ch % 2, :], ps[:, x_bank(ch, kc), :], ACT.Copy).then_inc(xt_copied, 1)

            def sum_weight(w):
                act.wait_ge(f_in, 16 * (w + 1))
                nc.scalar.activation(tern[:, w, :], fraw[:, :], ACT.Abs, accum_out=wsum[:, w:w + 1]).then_inc(fsum_done, 1)
                act.wait_ge(fsum_done, w + 1)
                if w < 2:
                    act.dma_start(fraw_to(w + 1), f_dram[w + 1]).then_inc(f_in, 16)

            copy_x(0)
            for ch in range(CHUNKS):
                b, hs = ch // 2, ch % 2
                for before, j in zip((None,) + JOBS, JOBS + (None,)):
                    if j is not None:
                        np_ = P if j < 2 else DKV
                        act.wait_ge(proj_ready, 4 * ch + nth(j))
                        if ch:
                            act.wait_ge(pc_out[j], 16 * ch)
                        nc.scalar.activation(pcs[j][0:np_, 0, :], ps[0:np_, proj_bank(ch, j), :], ACT.Copy).then_inc(hi_done, 1)
                        if ch == 0 and before is None:
                            copy_x(1)
                    elif ch == 0:
                        act.wait_ge(mw_in, 16)
                        nc.scalar.activation(w1[:, 1:2], w1[:, 0:1], ACT.Exp, scale=-1.0).then_inc(w_step, 1)
                    if before is not None:
                        np_ = P if before < 2 else DKV
                        act.wait_ge(rest_done, 3 * ch + nth(before))
                        nc.scalar.activation(pcs[before][0:np_, 1, :], rest[before][0:np_, :], ACT.Copy).then_inc(mid_done, 1)
                act.wait_ge(proj_ready, 4 * ch + 4)
                nc.scalar.activation(vop[:, b, hs * TPC:(hs + 1) * TPC, :, 0:DH],
                                     ps[:, proj_bank(ch, 3), 0:TPC * DKV].rearrange("p (t h d) -> p t h d", t=TPC, h=NH),
                                     ACT.Copy).then_inc(v_done, 1)
                for j in range(2):
                    if ch:
                        act.wait_ge(sig_done, 2 * (ch - 1) + j + 1)
                    nc.scalar.activation(elu_e[j][:, :], ps[:, proj_bank(ch, j), :], ACT.Relu, scale=-1.0).then_inc(neg_done, 1)
                for j in range(2):
                    act.wait_ge(neg_done, 2 * ch + j + 1)
                    nc.scalar.activation(elu_e[j][:, :], elu_e[j][:, :], ACT.Exp, scale=-1.0).then_inc(exp_done, 1)
                if ch:
                    sum_weight(ch - 1)
                if ch in (1, 2):
                    copy_x(ch + 1)
            act.dma_start(fraw_to(0), f_dram[0]).then_inc(f_in2, 16)

            def high_pieces(g):
                for kc in range(KC):
                    act.wait_ge(zt_ready, KC * g + kc + 1)
                    if g >= 2:
                        act.wait_ge(gate_ready, ER * (g - 1))
                    nc.scalar.activation(zp[:, g % 2, 0, kc, :], ps[:, zbank(g, kc), :], ACT.Copy).then_inc(zhi_done, 1)

            def save_acc(i, c):
                q = 4 * i + c
                act.wait_ge(pv_done, TILES * (q + 1))
                if not (isinstance(i, int) and q < 2):
                    act.wait_ge(sel_ready, q - 1)
                nc.scalar.activation(acc_sb[:, c % 2, :], ps[:, ACC, :], ACT.Copy).then_inc(acc_saved, 1)

            def quad(i, c):
                q = 4 * i + c
                first = isinstance(i, int) and q == 0
                for t in range(TILES):
                    act.wait_ge(score_b, TILES * q + t + 1)
                    if not (first and t < PSLOTS):
                        act.wait_ge(pv_done, TILES * q + t + 1 - PSLOTS)
                    nc.scalar.activation(prob[:, t % PSLOTS, :], ps[:, 4 + slot_of(t) % 3, :], ACT.Exp,
                                         scale=SCALE).then_inc(prob_done, 1)
                    if t == HG - 1 and not first:
                        save_acc(*at(i, c, -1))
                    if t == MISC_SLOT and is_last(i) and c == 3:
                        high_pieces(0)
                if isinstance(i, int) and i == 0 and c in (1, 3):
                    act.wait_ge(tern_step, 3 * (c // 2) + 2)
                    act.dma_start(fraw_to(c // 2 + 1), f_dram[c // 2 + 1]).then_inc(f_in2, 16)

            all_quads(act, quad)
            save_acc(ITERS - 1, 3)

            def high_hidden(n):
                g = n // ER
                act.wait_ge(hid_done, n + 1)
                if g >= 2:
                    act.wait_ge(down_ready, 2 * (g - 1))
                nc.scalar.activation(hp[:, g % 2, 0, n % ER, :], hid[n % 3][:, :], ACT.Copy).then_inc(hhi_done, 1)

            for g in range(CHUNKS):
                for r in range(ER):
                    n = ER * g + r
                    act.wait_ge(up_ready, n + 1)
                    if n >= 2:
                        act.wait_ge(hid_done, n - 1)
                    nc.scalar.activation(silu[r % 2][:, :], ps[:, r % 2, :], ACT.Silu,
                                         scale=wscale[:, 0, 0:1]).then_inc(silu_done, 1)
                    if n:
                        high_hidden(n - 1)
                    if r == 3 and g + 1 < CHUNKS:
                        high_pieces(g + 1)
            high_hidden(ER * CHUNKS - 1)

        @block.vector
        def _(dve):
            v = nc.vector
            v.memset(qop[64:MAX_ROW, :, :, :].rearrange("r c h s -> r (c h s)").bitcast(F32), 0.0).then_inc(zero_rows, 1)
            v.memset(kop[64:MAX_ROW, :, :, :].rearrange("r b h s -> r (b h s)").bitcast(F32), 0.0).then_inc(zero_rows, 1)

            def memory_weight_sigmoid():
                dve.wait_ge(w_step, 1)
                v.tensor_scalar(w1[:, 1:2], w1[:, 1:2], 1.0, None, ALU.add).then_inc(w_step, 1)
                dve.wait_ge(w_step, 2)
                v.reciprocal(w1[:, 2:3], w1[:, 1:2]).then_inc(w_step, 1)
                dve.wait_ge(w_step, 3)
                v.tensor_scalar(w1[:, 3:4], w1[:, 2:3], -1.0, 1.0, ALU.mult, ALU.add).then_inc(w_step, 1)
                dve.wait_ge(mem_in, 64)
                v.tensor_scalar(memd[:, 0:P], memd[:, 0:P], w1[:, 2:3], None, ALU.mult).then_inc(w_step, 1)

            def scale_mem(ch, st):
                n = TPC * ch + st
                num = ps[:, mem_bank(ch, st), 0:260].rearrange("p (f c) -> p f c", f=2)
                dve.wait_ge(mem_ready, n + 1)
                rm = rmem[:, n % 2, :].rearrange("p (f m) -> p f m", f=2)
                v.reciprocal(rm, num[:, :, P:P + 2]).then_inc(rm_step, 1)
                dve.wait_ge(rm_step, n + 1)
                if n >= 2:
                    dve.wait_ge(xr_done, n - 1)
                v.tensor_tensor(amem[:, n % 2, :].rearrange("p (f m k) -> p f m k", f=2, m=2),
                                num[:, :, 0:P].rearrange("p f (m k) -> p f m k", m=2),
                                rm.unsqueeze(3).broadcast_to([P, 2, 2, DKV]), ALU.mult).then_inc(mem_scaled, 1)

            def take_rest(ch, j):
                np_ = P if j < 2 else DKV
                dve.wait_ge(hi_done, 3 * ch + nth(j))
                if ch:
                    dve.wait_ge(lo_done, 3 * (ch - 1) + nth(j))
                v.tensor_tensor(rest[j][0:np_, :], ps[0:np_, proj_bank(ch, j), :], pcs[j][0:np_, 0, :], ALU.subtract).then_inc(rest_done, 1)

            def elu(ch):
                for j in range(2):
                    dve.wait_ge(exp_done, 2 * ch + j + 1)
                    v.tensor_scalar(elu_e[j][:, :], elu_e[j][:, :], -1.0, None, ALU.add).then_inc(em_done, 1)
                for j in range(2):
                    dve.wait_ge(em_done, 2 * ch + j + 1)
                    v.scalar_tensor_tensor(out=sig[j][:, :], in0=ps[:, proj_bank(ch, j), :], scalar=0.0, in1=elu_e[j][:, :],
                                           op0=ALU.max, op1=ALU.add).then_inc(sig_done, 1)

            def take_max(i, c, pairs):
                q = 4 * i + c
                for p in pairs:
                    dve.wait_ge(score_a, PAIRS * q + p + 1)
                    if p == 0 and not (isinstance(i, int) and q < 2):
                        dve.wait_ge(split_step, 4 * (q - 1))
                    v.tensor_reduce(mx[:, c % 2, p:p + 1], ps[:, 2 * (p % 2):2 * (p % 2) + 2, :],
                                    AX.XY, ALU.max, negate=True).then_inc(max_done, 1)

            def early_max(k):
                take_max(0, k // PAIRS, [k % PAIRS])

            def copy_mt(i, c, bank=MISC):
                q = 4 * i + c
                dve.wait_ge(mt_ready, q + 1)
                if not (isinstance(i, int) and q < 2):
                    if isinstance(i, int) and i == 0:
                        dve.wait_ge(mrow_in[(c - 2) % 4], 16)
                    elif c >= 2:
                        dve.wait_ge(mrow_in[c - 2], 16 * (i + 1))
                    else:
                        dve.wait_ge(mrow_in[c + 2], 16 * i)
                v.tensor_copy(mrow[:, c % 2, :], ps[0:PIECES * PAIRS, bank, 0:P // 2].bitcast(BF16)).then_inc(mt_copied, 1)

            def normalize(i, c):
                q = 4 * i + c
                sel = ps[:, MISC, SEL0:SEL0 + TPC * SELW].rearrange("p (t h w) -> p t h w", t=TPC, w=VW // 2)[:, :, 0:2 * HG - 1:2, :]
                dve.wait_ge(sel_ready, q + 1)
                v.reciprocal(rden[:, :, :], sel[:, :, :, DH]).then_inc(rden_done, 1)
                dve.wait_ge(rden_done, q + 1)
                v.tensor_tensor(attn[:, i, c // 2, :, HG * DH * (c % 2):HG * DH * (c % 2 + 1)].rearrange("p t (h d) -> p t h d", h=HG),
                                sel[:, :, :, 0:DH], rden[:, :, :].unsqueeze(3).broadcast_to([P, TPC, HG, DH]),
                                ALU.mult).then_inc(sel_used, 1)

            def quad(i, c):
                split = MISC_SLOT // 2 - PAIRS // 2
                if exists(i, c, 1):
                    take_max(*at(i, c, 1), range(PAIRS // 2, PAIRS))
                if exists(i, c, 2):
                    take_max(*at(i, c, 2), range(0, split))
                if exists(i, c, 1):
                    copy_mt(*at(i, c, 1))
                if not is_first(i, c):
                    normalize(*at(i, c, -1))
                if exists(i, c, 2):
                    take_max(*at(i, c, 2), range(split, PAIRS // 2))
                if is_last(i) and c == 2:
                    copy_weights(0, 4)
                    norm_attention(0)
                    norm_attention(1)
                if is_last(i) and c == 3:
                    copy_weights(4, 2)
                    rest_pieces(0)
                    norm_attention(2)

            def copy_weights(k, n):
                for k in range(k, k + n):
                    dve.wait_ge(tt_ready, k + 1)
                    if k < 4:
                        dst, fine = upT[:, k // 2, k % 2, :], upT_fine[:, k // 2, k % 2, :]
                    else:
                        dst, fine = (t[:, 4 * (k - 4):4 * (k - 3), :].rearrange("p r d -> p (r d)") for t in (downT, downT_fine))
                    v.tensor_copy(dst, ps[:, k % 4, :].bitcast(BF16)).then_inc(tt_copied, 1)
                    dve.wait_ge(tt_copied, k + 1)
                    v.tensor_scalar(fine, dst, FINE, None, ALU.mult).then_inc(fine_done, 1)

            def norm_stats(n, y, sts):
                before = 8 * n if n < 8 else 8 * n - 4
                for st in sts:
                    v.bn_stats(stat[:, st, :], y[:, st, :]).then_inc(stat_done, 1)
                dve.wait_ge(stat_done, before + len(sts))
                for st in sts:
                    v.bn_aggr(mv[:, st, :], stat[:, st, :]).then_inc(stat_done, 1)
                dve.wait_ge(stat_done, before + 2 * len(sts))
                v.tensor_scalar(rstd[:, sts.start:sts.stop], mv[:, sts.start:sts.stop, 1], LN_EPS, None, ALU.add).then_inc(var_done, 1)

            def norm_apply(n, y, dst, done, sts):
                dve.wait_ge(rstd_done, n + 1)
                for st in sts:
                    v.tensor_scalar(dst[:, st, :], y[:, st, :], mv[:, st, 0:1], rstd[:, st:st + 1],
                                    ALU.subtract, ALU.mult).then_inc(done, 1)

            def add_attention(g):
                b, hs, tiles = chunk(g)
                y = xr[:, tiles, :]
                dve.wait_ge(sel_used, (30, 30, 31, QUADS)[g])
                for st in range(TPC):
                    yt = y[:, st, :].rearrange("p (n k) -> p n k", n=NQ)
                    v.scalar_tensor_tensor(out=yt, in0=attn[:, NQ * hs:NQ * (hs + 1), b, st, :], scalar=w1[:, 3:4], in1=yt,
                                           op0=ALU.mult, op1=ALU.add).then_inc(y_done, 1)

            def attention_stats(g):
                dve.wait_ge(y_done, TPC * (g + 1))
                norm_stats(g, xr[:, chunk(g)[2], :], range(TPC))

            def attention_apply(g):
                y = xr[:, chunk(g)[2], :]
                norm_apply(g, y, y, z_done, range(TPC))

            def norm_attention(g):
                add_attention(g)
                attention_stats(g)
                attention_apply(g)

            def rest_pieces(g):
                for kc in range(KC):
                    dve.wait_ge(zhi_done, KC * g + kc + 1)
                    if g:
                        dve.wait_ge(zp_done, KC * g)
                    v.tensor_tensor(zc[:, kc, :], ps[:, zbank(g, kc), :], zp[:, g % 2, 0, kc, :], ALU.subtract).then_inc(zrest_done, 1)

            def make_hidden(n):
                if n < ER * CHUNKS:
                    dve.wait_ge(gate_ready, n + 1)
                    dve.wait_ge(silu_done, n + 1)
                    if n >= 3:
                        dve.wait_ge(hlo_done, n - 2)
                    v.scalar_tensor_tensor(out=hid[n % 3][:, :], in0=ps[:, 2 + n % 2, :], scalar=hscale[:, 2:3],
                                           in1=silu[n % 2][:, :], op0=ALU.mult, op1=ALU.mult).then_inc(hid_done, 1)
                if n:
                    dve.wait_ge(hhi_done, n)
                    v.tensor_tensor(hid[(n - 1) % 3][:, :], hid[(n - 1) % 3][:, :], hp[:, (n - 1) // ER % 2, 0, (n - 1) % ER, :],
                                    ALU.subtract).then_inc(hrest_done, 1)

            def add_down(g, h):
                _, _, tiles = chunk(g)
                dve.wait_ge(down_ready, 2 * g + h + 1)
                zh = xr[:, tiles, :][:, 2 * h:2 * h + 2, :]
                product = ps[:, DOWN_BANKS[h], :].rearrange("p (t d) -> p t d", t=2) if g + 1 < CHUNKS else ps[:, 4 + 2 * h:6 + 2 * h, 0:DM]
                v.scalar_tensor_tensor(out=zh, in0=product,
                                       scalar=hscale[:, 3:4], in1=zh,
                                       op0=ALU.mult, op1=ALU.add).then_inc(y2_done, 1)

            def out_stats(g, sts):
                dve.wait_ge(y2_done, 2 * g + sts.stop // 2)
                norm_stats(CHUNKS + g + (sts.start > 0), xr[:, chunk(g)[2], :], range(sts.start, sts.stop))

            def out_apply(g, sts):
                b, _, tiles = chunk(g)
                if g >= 2:
                    dve.wait_ge(out_done[b], 16)
                norm_apply(CHUNKS + g + (sts.start > 0), xr[:, tiles, :], yout[:, b, :, :], yout_done, range(sts.start, sts.stop))

            for j in JOBS:
                take_rest(0, j)
            memory_weight_sigmoid()
            elu(0)
            for j in JOBS:
                take_rest(1, j)
            for st in range(TPC):
                scale_mem(0, st)
            elu(1)
            early_max(0)
            for st in range(TPC):
                early_max(1 + st)
                scale_mem(1, st)
            for k in (5, 6, 7):
                early_max(k)
            for p, j in enumerate(JOBS):
                early_max(8 + p)
                take_rest(2, j)
            early_max(11)
            early_max(12)
            elu(2)
            for st in range(TPC):
                early_max(13 + st)
                scale_mem(2, st)
            early_max(17)
            copy_mt(0, 0, 2)
            early_max(18)
            for p, j in enumerate(JOBS):
                take_rest(3, j)
                early_max(19 + p)
            early_max(22)
            elu(3)
            early_max(23)
            for st in range(TPC):
                scale_mem(3, st)
                if st == 0:
                    dve.wait_ge(fsum_all, 1)
                    v.tensor_scalar(wscale[:, :, 0], ps[:, MISC, 0:3], 1.0 / (DE * DM), Q_EPS, ALU.mult, ALU.add).then_inc(fscale_step, 1)
            dve.wait_ge(fscale_step, 1)
            v.tensor_scalar(wscale[:, :, 1], wscale[:, :, 0], 0.5, None, ALU.mult).then_inc(fscale_step, 1)
            v.tensor_scalar(wscale[:, :, 2], wscale[:, :, 0], -0.5, None, ALU.mult).then_inc(fscale_step, 1)
            v.reciprocal(hscale[:, 0:1], wscale[:, 0, 0:1]).then_inc(fscale_step, 1)
            v.tensor_tensor(hscale[:, 1:2], wscale[:, 0, 0:1], wscale[:, 1, 0:1], ALU.mult).then_inc(fscale_step, 1)
            dve.wait_ge(fscale_step, 5)
            v.tensor_scalar(hscale[:, 2:3], hscale[:, 0:1], HID, None, ALU.mult).then_inc(fscale_step, 1)
            v.tensor_scalar(hscale[:, 3:4], hscale[:, 1:2], wscale[:, 2, 0:1], 1.0 / HID, ALU.mult, ALU.mult).then_inc(fscale_step, 1)
            all_quads(dve, quad)

            full = slice(0, TPC)
            dve.wait_ge(fscale_step, 7)
            for g in range(CHUNKS):
                for r in range(4):
                    make_hidden(ER * g + r)
                if g:
                    for h in range(2):
                        add_down(g - 1, h)
                if g + 1 < CHUNKS:
                    rest_pieces(g + 1)
                make_hidden(ER * g + 4)
                if g == 0:
                    normalize(ITERS - 1, 3)
                    add_attention(3)
                make_hidden(ER * g + 5)
                if g:
                    out_stats(g - 1, full)
                else:
                    attention_stats(3)
                make_hidden(ER * g + 6)
                make_hidden(ER * g + 7)
                if g:
                    out_apply(g - 1, full)
                else:
                    attention_apply(3)
            make_hidden(ER * CHUNKS)
            for h, sts in enumerate(out_parts(CHUNKS - 1)):
                add_down(CHUNKS - 1, h)
                out_stats(CHUNKS - 1, sts)
            for sts in out_parts(CHUNKS - 1):
                out_apply(CHUNKS - 1, sts)

        @block.tensor
        def _(pe):
            pe.wait_ge(ident_ready, 2)
            pe.wait_ge(w_in, 48)
            for kc in range(KC):
                for f in range(3):
                    last = pe.transpose(ps[:, kc, P * f:P * (f + 1)], wraw[:, f, P * kc:P * (kc + 1)], identf[:, :])
                last.then_inc(wt_ready, 1)

            def read_memory(ch, st):
                n = TPC * ch + st
                if st == 0:
                    pe.wait_ge(w_step, 5)
                    pe.wait_ge(sig_done, 2 * ch + 2)
                if ch and st == 0:
                    pe.wait_ge(rest_done, 3 * ch + 3)
                    pe.wait_ge(v_done, ch + 1)
                elif n >= 2:
                    pe.wait_ge(mem_scaled, n - 1)
                for f in range(2):
                    last = pe.matmul(ps[:, mem_bank(ch, st), 130 * f:130 * (f + 1)], sig[f][:, P * st:P * (st + 1)],
                                     memd[:, :], start=True, stop=True)
                last.then_inc(mem_ready, 1)

            def turn_x(ch, kc):
                pe.wait_ge(x_in[ch], 16)
                if ch == 0:
                    pe.wait_ge(wt_copied, 2 * (kc + 1))
                elif ch == 1:
                    pe.wait_ge(xt_copied, kc + 1)
                else:
                    pe.wait_ge(mem_scaled, TPC * ch)
                for st in range(TPC):
                    last = pe.transpose(ps[:, x_bank(ch, kc), P * st:P * (st + 1)], xr[:, TPC * ch + st, P * kc:P * (kc + 1)], identf[:, :])
                last.then_inc(xt_ready, 1)

            def project(ch, j):
                np_ = P if j < 2 else DKV
                if nth(j) == 1:
                    pe.wait_ge(xt_copied, KC * (ch + 1))
                if j < 2 and ch >= 2:
                    pe.wait_ge(sig_done, 2 * (ch - 1) + j + 1)
                if j == 2 and ch == 1:
                    pe.wait_ge(rest_done, 3)
                for kc in range(KC):
                    last = pe.matmul(ps[0:np_, proj_bank(ch, j), :], WT[:, kc, P * j:P * j + np_], xT[:, kc, ch % 2, :],
                                     start=(kc == 0), stop=(kc == KC - 1))
                last.then_inc(proj_ready, 1)

            def project_v(ch):
                if ch == 1:
                    pe.wait_ge(v_done, 1)
                for st in range(TPC):
                    for kc in range(KC):
                        last = pe.matmul(ps[:, proj_bank(ch, 3), DKV * st:DKV * (st + 1)], xT[:, kc, ch % 2, P * st:P * (st + 1)],
                                         WT[:, kc, 2 * P + DKV:3 * P], start=(kc == 0), stop=(kc == KC - 1))
                last.then_inc(proj_ready, 1)

            def max_scores(i, c, pairs):
                q, b, hg = 4 * i + c, c // 2, c % 2
                for p in pairs:
                    j, st = p // TPC, p % TPC
                    if p == 0:
                        pe.wait_ge(qop_in[c], 16 * PIECES * (i + 1))
                        if isinstance(i, int) and i == 0:
                            pe.wait_ge(kop_in[c], 16 * PIECES)
                    if not (is_first(i, c) and p < 2):
                        pe.wait_ge(max_done, PAIRS * q + p - 1)
                    for half in range(2):
                        last = pe.matmul(ps[:, 2 * (p % 2) + half, :], qop[0:MAX_ROW, c, j, P * st:P * (st + 1)],
                                         kop[0:MAX_ROW, b, HG * hg + j, HALF * half:HALF * (half + 1)], start=True, stop=True)
                    last.then_inc(score_a, 1)

            def early_scores(k):
                max_scores(0, k // PAIRS, [k % PAIRS])

            def turn_max(i, c, bank=MISC):
                q = 4 * i + c
                pe.wait_ge(split_step, 4 * (q + 1))
                pe.transpose(ps[:, bank, 0:P // 2].bitcast(BF16), mpc[:, c % 2, :], identb[:, :]).then_inc(mt_ready, 1)

            def misc_read(i, c):
                if exists(i, c, 1):
                    pe.wait_ge(mt_copied, 4 * i + c + 2)
                if not is_first(i, c):
                    pe.wait_ge(sel_used, 4 * i + c)

            def scores(i, c, t):
                q, b, hg, tb, j = 4 * i + c, c // 2, c % 2, t // HG, t % HG
                if t == 0:
                    if isinstance(i, int) and i == 0 and c % 2 == 0:
                        pe.wait_ge(ops_set, 3 * (b + 1))
                    pe.wait_ge(mrow_in[c], 16 * (i + 1))
                before = slot_of(t) - 3
                if before == MISC_SLOT:
                    misc_read(i, c)
                elif before >= 0 or not is_first(i, c):
                    pe.wait_ge(prob_done, TILES * q + before + 1 - (before > MISC_SLOT))
                pe.matmul(ps[:, 4 + slot_of(t) % 3, :], kop[0:ROWS, b, HG * hg + j, P * tb:P * (tb + 1)],
                          qop[0:ROWS, c, j, :], start=True, stop=True).then_inc(score_b, 1)

            def times_v(i, c, tb):
                q, b, hg = 4 * i + c, c // 2, c % 2
                if tb == 0:
                    if not is_first(i, c):
                        pe.wait_ge(acc_saved, q)
                for j in range(HG):
                    t = HG * tb + j
                    pe.wait_ge(prob_done, TILES * q + t + 1)
                    pe.matmul(ps[VW * j:VW * (j + 1), ACC, :], vop[:, b, tb, HG * hg + j, :], prob[:, t % PSLOTS, :],
                              start=(tb == 0), stop=(tb == TB - 1)).then_inc(pv_done, 1)

            def down_last(g):
                pe.wait_ge(y2_done, 2 * g)
                pe.wait_ge(zrest_done, KC * CHUNKS)
                for r in range(ER):
                    pe.wait_ge(hlo_done, ER * g + r + 1)
                    for st in range(TPC):
                        for e, wt in ((0, downT), (1, downT_fine)):
                            last = pe.matmul(ps[:, 4 + st, 0:DM], hp[:, g % 2, e, r, P * st:P * (st + 1)], wt[:, r, :],
                                             start=(r == 0 and e == 0), stop=(r == ER - 1 and e == 1))
                        if r == ER - 1 and st % 2:
                            last.then_inc(down_ready, 1)

            def select(i, c):
                q = 4 * i + c
                pe.wait_ge(acc_saved, q + 1)
                for st in range(TPC):
                    last = pe.transpose(ps[:, MISC, SEL0 + SELW * st:SEL0 + SELW * (st + 1)],
                                        acc_sb[0:SELW, c % 2, P * st:P * (st + 1)], identf[0:SELW, 0:SELW])
                last.then_inc(sel_ready, 1)

            def quad(i, c):
                for tb in range(TB):
                    ahead, first = (1, PAIRS // 2 + 2 * tb) if tb < TB // 2 else (2, 2 * tb - TB)
                    scores(i, c, HG * tb)
                    if exists(i, c, ahead):
                        max_scores(*at(i, c, ahead), [first])
                    scores(i, c, HG * tb + 1)
                    scores(i, c, HG * tb + 2)
                    if exists(i, c, ahead):
                        max_scores(*at(i, c, ahead), [first + 1])
                    scores(i, c, HG * tb + 3)
                    if is_last(i) and c == 2 and tb in (4, 6):
                        turn_up_gate(tb // 2 - 2)
                    if is_last(i) and c == 3 and tb == 1:
                        turn_down()
                    if is_last(i) and c == 3 and tb == 2:
                        turn_rows(0)
                    if HG * (tb + 1) == MISC_SLOT:
                        pe.wait_ge(prob_done, TILES * (4 * i + c) + MISC_SLOT - 2)
                        if not is_first(i, c):
                            select(*at(i, c, -1))
                        if exists(i, c, 1):
                            turn_max(*at(i, c, 1))
                    if tb:
                        times_v(i, c, tb - 1)
                    elif not is_first(i, c):
                        times_v(*at(i, c, -1), TB - 1)

            def turn_up_gate(w):
                pe.wait_ge(tern_step, 9)
                pe.wait_ge(max_done, PAIRS * QUADS)
                for kc in range(KC):
                    for r in range(ER):
                        last = pe.transpose(ps[:, KC * w + kc, :].bitcast(BF16)[:, P * r:P * (r + 1)],
                                            tern[:, w, DM * r + P * kc:DM * r + P * (kc + 1)], identb[:, :])
                    last.then_inc(tt_ready, 1)

            def turn_down():
                pe.wait_ge(tt_copied, 2)
                tdown = tern[:, 2, :].rearrange("p (k e r) -> p k e r", k=KC, r=ER)
                for h in range(2):
                    for r in range(4):
                        for kc in range(KC):
                            last = pe.transpose(ps[:, h, :].bitcast(BF16)[:, DM * r + P * kc:DM * r + P * (kc + 1)],
                                                tdown[:, kc, :, 4 * h + r], identb[:, :])
                    last.then_inc(tt_ready, 1)

            def turn_rows(g):
                _, _, tiles = chunk(g)
                pe.wait_ge(z_done, TPC * (g + 1))
                if g == 0:
                    pe.wait_ge(tt_copied, 4)
                elif g > 1:
                    pe.wait_ge(zrest_done, KC * g)
                for kc in range(KC):
                    for st in range(TPC):
                        last = pe.transpose(ps[:, zbank(g, kc), P * st:P * (st + 1)],
                                            xr[:, tiles, :][:, st, P * kc:P * (kc + 1)], identf[:, :])
                    last.then_inc(zt_ready, 1)

            def up_gate(g, rs):
                for r in rs:
                    n = ER * g + r
                    if r == 0:
                        pe.wait_ge(zp_done, KC * (g + 1))
                    if n == 0:
                        pe.wait_ge(fine_done, 6)
                    if n >= 2:
                        pe.wait_ge(hid_done, n - 1)
                    for w, ready in ((0, up_ready), (1, gate_ready)):
                        for kc in range(KC):
                            for e, wt in ((0, upT), (1, upT_fine)):
                                last = pe.matmul(ps[:, 2 * w + r % 2, :], wt[:, w, kc, P * r:P * (r + 1)], zp[:, g % 2, e, kc, :],
                                                 start=(kc == 0 and e == 0), stop=(kc == KC - 1 and e == 1))
                        last.then_inc(ready, 1)

            def down(g):
                pe.wait_ge(hlo_done, ER * (g + 1))
                if g:
                    pe.wait_ge(y2_done, 2 * g)
                else:
                    pe.wait_ge(sel_used, QUADS)
                    pe.wait_ge(acc_saved, QUADS)
                for st in range(TPC):
                    for r in range(ER):
                        for e, wt in ((0, downT), (1, downT_fine)):
                            last = pe.matmul(ps[:, DOWN_BANKS[st // 2], DM * (st % 2):DM * (st % 2 + 1)],
                                             hp[:, g % 2, e, r, P * st:P * (st + 1)], wt[:, r, :],
                                             start=(r == 0 and e == 0), stop=(r == ER - 1 and e == 1))
                    if st % 2:
                        last.then_inc(down_ready, 1)

            for kc in range(KC):
                turn_x(0, kc)
            project(0, JOBS[0])
            for kc in range(KC):
                turn_x(1, kc)
            for j in JOBS[1:]:
                project(0, j)
            project_v(0)
            for j in JOBS:
                project(1, j)
            project_v(1)
            for st in range(TPC):
                read_memory(0, st)
            pe.wait_ge(mem_scaled, TPC)
            pe.wait_ge(sig_done, 2)
            early_scores(0)
            for st in range(TPC):
                early_scores(1 + st)
                read_memory(1, st)
            for kc in range(KC):
                early_scores(5 + kc)
                turn_x(2, kc)
            for p, j in enumerate(JOBS):
                early_scores(7 + p)
                project(2, j)
            early_scores(10)
            project_v(2)
            early_scores(11)
            early_scores(12)
            for st in range(TPC):
                early_scores(13 + st)
                read_memory(2, st)
            early_scores(17)
            for kc in range(KC):
                turn_x(3, kc)
            early_scores(18)
            pe.wait_ge(const_ready, CONSTS)
            pe.wait_ge(max_done, 18)
            turn_max(0, 0, 2)
            project(3, JOBS[0])
            pe.wait_ge(mt_copied, 1)
            early_scores(19)
            for p in (1, 2):
                project(3, JOBS[p])
                early_scores(19 + p)
            project_v(3)
            early_scores(22)
            early_scores(23)
            for st in range(TPC):
                read_memory(3, st)
                if st == 0:
                    pe.wait_ge(fsum_done, 3)
                    pe.matmul(ps[:, MISC, 0:3], ones[:, :], wsum[:, :], start=True, stop=True).then_inc(fsum_all, 1)
            pe.wait_ge(fscale_step, 1)
            pe.wait_ge(mem_scaled, TPC * CHUNKS)
            all_quads(pe, quad)
            times_v(ITERS - 1, 3, TB - 1)
            pe.wait_ge(prob_done, TILES * QUADS)

            for g in range(CHUNKS):
                up_gate(g, range(0, 4))
                if g:
                    down(g - 1)
                else:
                    select(ITERS - 1, 3)
                if g + 1 < CHUNKS:
                    turn_rows(g + 1)
                up_gate(g, range(4, ER))
            down_last(CHUNKS - 1)


_INS = ["L0_attn_x", "L0_attn_Wq", "L0_attn_Wk", "L0_attn_Wv", "L0_attn_memory", "L0_attn_memory_norm",
        "L0_attn_memory_weight", "L0_ffn_W_up", "L0_ffn_W_gate", "L0_ffn_W_down"]


def kernel(**inputs):
    import numpy as _np
    import concourse.bacc as _bacc
    from concourse import mybir as _mybir
    from concourse.bass_utils import run_bass_kernel_spmd as _run

    nc = _bacc.Bacc("TRN2", target_bir_lowering=False, num_devices=1)
    arrays, args = {}, []
    for name in _INS:
        a = _np.ascontiguousarray(inputs[name])
        arrays[f"in_{name}"] = a
        args.append(nc.dram_tensor(f"in_{name}", a.shape, _mybir.dt.from_np(a.dtype), kind="ExternalInput").ap())
    args.append(nc.dram_tensor("out_0", (2, 1024, 256), _mybir.dt.float32, kind="ExternalOutput").ap())
    attention_ffn_kernel(nc, *args)
    r = _run(nc, [arrays], core_ids=[0])
    return r.results[0]["out_0"]
```
